# Optimizing a Trainium2 kernel written in Bass

```python
import numpy as np
import jax
import jax.numpy as jnp

def _softmax(x, axis=-1):
    return jax.nn.softmax(x, axis=axis)

def _gelu(x):
    return jax.nn.gelu(x, approximate=True)

def _silu(x):
    return jax.nn.silu(x)

def _sigmoid(x):
    return jax.nn.sigmoid(x)

def _layernorm(x, axis=-1, eps=1e-05):
    m = jnp.mean(x, axis=axis, keepdims=True)
    v = jnp.var(x, axis=axis, keepdims=True)
    return (x - m) / jnp.sqrt(v + eps)

def _scatter_add(tgt, idx, src, axis=0):
    return tgt.at[idx].add(src)

def _segment_sum(src, seg, n):
    return jax.ops.segment_sum(src, seg, n)
kernel_name = 'mk_cond_resid_d4_seqx_r8_a60845'

def setup_inputs(seed: int=0):
    np.random.seed(seed)
    _w = jnp.asarray

    def _rec_inputs():
        import jax
        import jax.numpy as jnp
        _rk = jax.random.key(seed)
        x = -0.0002928 + 1 * jax.random.normal(jax.random.fold_in(_rk, 1), (4, 256, 128), jnp.float32)
        _lenS = 256 - jax.random.randint(jax.random.fold_in(_rk, 7), (4,), 0, max(1, 256 // 4) + 1, jnp.int32)
        _lenS2 = 256 - jax.random.randint(jax.random.fold_in(_rk, 8), (4,), 0, max(1, 256 // 4) + 1, jnp.int32)
        fside_16xSxS_0 = -5.72187e-05 + 0.999849 * jax.random.normal(jax.random.fold_in(_rk, 11), (16, 256, 256), jnp.float32)
        cond_64 = -0.0265395 + 0.99382 * jax.random.normal(jax.random.fold_in(_rk, 13), (4, 64), jnp.float32)
        _validS = jnp.arange(256)[None, :] < _lenS[:, None]
        _validS2 = jnp.arange(256)[None, :] < _lenS2[:, None]
        _causal = jnp.tril(jnp.ones((256, 256), dtype=bool))
        mask_BxS_bk0 = jnp.logical_not(jnp.broadcast_to(_validS[:, :], (4, 256)))
        mask_BxS_bf1 = jnp.ones((4, 256), dtype=bool)
        return (x, fside_16xSxS_0, cond_64, mask_BxS_bk0, mask_BxS_bf1)
    x, fside_16xSxS_0, cond_64, mask_BxS_bk0, mask_BxS_bf1 = _rec_inputs()

    def _L0_cond_setup():
        import jax, jax.numpy as jnp
        import numpy as np
        B, N, DIM, H, DH = (2, 256, 128, 16, 64)
        INNER = H * DH
        EPS = 1e-05

        def layernorm(x, g):
            mean = jnp.mean(x, axis=-1, keepdims=True)
            var = jnp.var(x, axis=-1, keepdims=True)
            return (x - mean) * jax.lax.rsqrt(var + EPS) * g
        key = jax.random.key(seed)
        ks = jax.random.split(key, 10)
        x = jax.random.normal(ks[0], (B, N, DIM), dtype=jnp.float32)
        attn_bias = jax.random.normal(ks[1], (H, N, N), dtype=jnp.float32)
        mask = jax.random.randint(ks[2], (B, N), 0, 2).astype(bool)
        g_in = jnp.ones((DIM,), dtype=jnp.float32)
        null_attn_bias = jax.random.normal(ks[3], (H,), dtype=jnp.float32)
        null_kv = jax.random.normal(ks[4], (2, DH), dtype=jnp.float32)
        Wq = jax.random.normal(ks[5], (DIM, INNER), dtype=jnp.float32) * 0.02
        Wkv = jax.random.normal(ks[6], (DIM, 2 * DH), dtype=jnp.float32) * 0.02
        Wo = jax.random.normal(ks[7], (INNER, DIM), dtype=jnp.float32) * 0.02
        g_out = jnp.ones((DIM,), dtype=jnp.float32)
        return {'x': x, 'attn_bias': attn_bias, 'mask': mask, 'g_in': g_in, 'null_attn_bias': null_attn_bias, 'null_kv': null_kv, 'Wq': Wq, 'Wkv': Wkv, 'Wo': Wo, 'g_out': g_out}
    _L0_cond_all = _L0_cond_setup()
    _L0_cond_in = {k: v for k, v in _L0_cond_all.items() if k in ('g_in', 'null_attn_bias', 'Wq', 'Wkv', 'Wo', 'g_out')}
    del _L0_cond_all

    def _L1_cond_setup():
        import jax, jax.numpy as jnp
        import numpy as np
        DIM = 128
        HEADS = 16
        DIM_HEAD = 64
        SCALE = 8.0

        def ln(x, g, eps=1e-05):
            mean = x.mean(axis=-1, keepdims=True)
            var = ((x - mean) ** 2).mean(axis=-1, keepdims=True)
            return (x - mean) * jax.lax.rsqrt(var + eps) * g

        def l2norm(t):
            n = jnp.maximum(jnp.linalg.norm(t, axis=-1, keepdims=True), 1e-12)
            return t / n

        def rel_pos_bias(n, w0, b0, g0, w1, b1, g1, w2, b2, dtype):
            pos = jnp.arange(-n + 1, n, dtype=dtype)[:, None]
            h = jax.nn.silu(ln(pos @ w0 + b0, g0))
            h = jax.nn.silu(ln(h @ w1 + b1, g1))
            h = h @ w2 + b2
            i = jnp.arange(n)
            idx = i[:, None] - i[None, :] + n - 1
            bias = h[idx]
            return jnp.transpose(bias, (2, 0, 1))
        key = jax.random.key(seed)
        ks = jax.random.split(key, 16)
        b, n = (2, 256)
        inner = HEADS * DIM_HEAD
        s = 0.02
        return {'x': jax.random.normal(ks[0], (b, n, DIM), jnp.float32), 'mask': jnp.ones((b, n), dtype=bool), 'g_norm': jnp.ones((DIM,), jnp.float32), 'Wq': jax.random.normal(ks[1], (DIM, inner), jnp.float32) * s, 'Wkv': jax.random.normal(ks[2], (DIM, 2 * DIM_HEAD), jnp.float32) * s, 'q_scale': jnp.ones((DIM_HEAD,), jnp.float32), 'k_scale': jnp.ones((DIM_HEAD,), jnp.float32), 'null_kv': jax.random.normal(ks[3], (2, DIM_HEAD), jnp.float32), 'null_attn_bias': jax.random.normal(ks[4], (HEADS,), jnp.float32), 'w0': jax.random.normal(ks[5], (1, DIM), jnp.float32) * s, 'b0': jnp.zeros((DIM,), jnp.float32), 'g0': jnp.ones((DIM,), jnp.float32), 'w1': jax.random.normal(ks[6], (DIM, DIM), jnp.float32) * s, 'b1': jnp.zeros((DIM,), jnp.float32), 'g1': jnp.ones((DIM,), jnp.float32), 'w2': jax.random.normal(ks[7], (DIM, HEADS), jnp.float32) * s, 'b2': jnp.zeros((HEADS,), jnp.float32), 'Wout': jax.random.normal(ks[8], (inner, DIM), jnp.float32) * s, 'g_out': jnp.ones((DIM,), jnp.float32)}
    _L1_cond_all = _L1_cond_setup()
    _L1_cond_in = {k: v for k, v in _L1_cond_all.items() if k in ('g_norm', 'Wq', 'Wkv', 'q_scale', 'k_scale', 'null_attn_bias', 'w0', 'b0', 'g0', 'w1', 'b1', 'g1', 'w2', 'b2', 'Wout', 'g_out')}
    del _L1_cond_all

    def _L2_cond_setup():
        import jax, jax.numpy as jnp
        import numpy as np
        B, S, H = (4, 256, 128)
        E = 8
        M = 64
        K = 2
        N_SHARED = 2
        SM = M * N_SHARED
        G = 64
        GE_TEMP = 1.0
        ALPHA = 0.001
        SEQ_AUX = True
        NORM_TOPK = True
        COS_TEMP = 0.78
        CONS_ALPHA = 0.01
        LEAKY_SLOPE = 0.01
        EPS_COS = 1e-08

        def _leaky(x):
            return jnp.where(x >= 0, x, LEAKY_SLOPE * x)

        def _moe_forward(hidden_states, g, wt, wg, w_gate, w_up, w_down, sw_gate, sw_up, sw_down):
            b, s, h = hidden_states.shape
            x = hidden_states.reshape(-1, h)
            T = x.shape[0]
            logits_h = x @ wt.T
            logits_g = g @ wg.T
            logits_g = jnp.repeat(logits_g, s, axis=0)
            logits = (logits_h + logits_g / GE_TEMP) / (1.0 + 1.0 / GE_TEMP)
            scores = jax.nn.softmax(logits, axis=-1)
            topk_w, topk_idx = jax.lax.top_k(scores, K)
            if K > 1 and NORM_TOPK:
                topk_w = topk_w / (topk_w.sum(-1, keepdims=True) + 1e-20)
            onehot = jax.nn.one_hot(topk_idx.reshape(b, s * K), E, dtype=jnp.float32)
            ce = onehot.sum(1) / (s * K / E)
            aux_loss = (ce * scores.reshape(b, s, E).mean(1)).sum(1).mean() * ALPHA
            gp = _leaky(jnp.einsum('th,ehm->etm', x, w_gate))
            up = jnp.einsum('th,ehm->etm', x, w_up)
            y_all = jnp.einsum('etm,emh->eth', gp * up, w_down)
            y_sel = y_all[topk_idx, jnp.arange(T)[:, None], :]
            y = (y_sel * topk_w[..., None]).sum(1).reshape(b, s, h)
            p = _leaky(hidden_states @ sw_gate) * (hidden_states @ sw_up) @ sw_down
            y = y + p
            num = jnp.sum(y * p, -1)
            den = jnp.maximum(jnp.linalg.norm(y, axis=-1), EPS_COS) * jnp.maximum(jnp.linalg.norm(p, axis=-1), EPS_COS)
            closs = CONS_ALPHA * jnp.mean(num / den / (1.0 + COS_TEMP))
            return (y, aux_loss + closs)
        key = jax.random.key(seed)
        ks = jax.random.split(key, 12)
        sh = 1.0 / np.sqrt(H)
        sm = 1.0 / np.sqrt(M)
        ssm = 1.0 / np.sqrt(SM)
        sg = 1.0 / np.sqrt(G)
        return {'hidden_states': jax.random.normal(ks[0], (B, S, H), jnp.float32), 'g': jax.random.normal(ks[1], (B, G), jnp.float32), 'wt': jax.random.uniform(ks[2], (E, H), jnp.float32, -sh, sh), 'wg': jax.random.uniform(ks[3], (E, G), jnp.float32, -sg, sg), 'w_gate': jax.random.uniform(ks[4], (E, H, M), jnp.float32, -sh, sh), 'w_up': jax.random.uniform(ks[5], (E, H, M), jnp.float32, -sh, sh), 'w_down': jax.random.uniform(ks[6], (E, M, H), jnp.float32, -sm, sm), 'sw_gate': jax.random.uniform(ks[7], (H, SM), jnp.float32, -sh, sh), 'sw_up': jax.random.uniform(ks[8], (H, SM), jnp.float32, -sh, sh), 'sw_down': jax.random.uniform(ks[9], (SM, H), jnp.float32, -ssm, ssm)}
    _L2_cond_all = _L2_cond_setup()
    _L2_cond_in = {k: v for k, v in _L2_cond_all.items() if k in ('wt', 'wg', 'w_gate', 'w_up', 'w_down', 'sw_gate', 'sw_up', 'sw_down')}
    del _L2_cond_all

    def _L3_cond_setup():
        import jax, jax.numpy as jnp
        import numpy as np
        B, S, H = (4, 256, 128)
        E = 8
        M = 64
        K = 2
        N_SHARED = 2
        SM = M * N_SHARED
        G = 64
        GE_TEMP = 1.0
        ALPHA = 0.001
        SEQ_AUX = True
        NORM_TOPK = True
        COS_TEMP = 0.78
        CONS_ALPHA = 0.01
        LEAKY_SLOPE = 0.01
        EPS_COS = 1e-08

        def _leaky(x):
            return jnp.where(x >= 0, x, LEAKY_SLOPE * x)

        def _moe_forward(hidden_states, g, wt, wg, w_gate, w_up, w_down, sw_gate, sw_up, sw_down):
            b, s, h = hidden_states.shape
            x = hidden_states.reshape(-1, h)
            T = x.shape[0]
            logits_h = x @ wt.T
            logits_g = g @ wg.T
            logits_g = jnp.repeat(logits_g, s, axis=0)
            logits = (logits_h + logits_g / GE_TEMP) / (1.0 + 1.0 / GE_TEMP)
            scores = jax.nn.softmax(logits, axis=-1)
            topk_w, topk_idx = jax.lax.top_k(scores, K)
            if K > 1 and NORM_TOPK:
                topk_w = topk_w / (topk_w.sum(-1, keepdims=True) + 1e-20)
            onehot = jax.nn.one_hot(topk_idx.reshape(b, s * K), E, dtype=jnp.float32)
            ce = onehot.sum(1) / (s * K / E)
            aux_loss = (ce * scores.reshape(b, s, E).mean(1)).sum(1).mean() * ALPHA
            gp = _leaky(jnp.einsum('th,ehm->etm', x, w_gate))
            up = jnp.einsum('th,ehm->etm', x, w_up)
            y_all = jnp.einsum('etm,emh->eth', gp * up, w_down)
            y_sel = y_all[topk_idx, jnp.arange(T)[:, None], :]
            y = (y_sel * topk_w[..., None]).sum(1).reshape(b, s, h)
            p = _leaky(hidden_states @ sw_gate) * (hidden_states @ sw_up) @ sw_down
            y = y + p
            num = jnp.sum(y * p, -1)
            den = jnp.maximum(jnp.linalg.norm(y, axis=-1), EPS_COS) * jnp.maximum(jnp.linalg.norm(p, axis=-1), EPS_COS)
            closs = CONS_ALPHA * jnp.mean(num / den / (1.0 + COS_TEMP))
            return (y, aux_loss + closs)
        key = jax.random.key(seed)
        ks = jax.random.split(key, 12)
        sh = 1.0 / np.sqrt(H)
        sm = 1.0 / np.sqrt(M)
        ssm = 1.0 / np.sqrt(SM)
        sg = 1.0 / np.sqrt(G)
        return {'hidden_states': jax.random.normal(ks[0], (B, S, H), jnp.float32), 'g': jax.random.normal(ks[1], (B, G), jnp.float32), 'wt': jax.random.uniform(ks[2], (E, H), jnp.float32, -sh, sh), 'wg': jax.random.uniform(ks[3], (E, G), jnp.float32, -sg, sg), 'w_gate': jax.random.uniform(ks[4], (E, H, M), jnp.float32, -sh, sh), 'w_up': jax.random.uniform(ks[5], (E, H, M), jnp.float32, -sh, sh), 'w_down': jax.random.uniform(ks[6], (E, M, H), jnp.float32, -sm, sm), 'sw_gate': jax.random.uniform(ks[7], (H, SM), jnp.float32, -sh, sh), 'sw_up': jax.random.uniform(ks[8], (H, SM), jnp.float32, -sh, sh), 'sw_down': jax.random.uniform(ks[9], (SM, H), jnp.float32, -ssm, ssm)}
    _L3_cond_all = _L3_cond_setup()
    _L3_cond_in = {k: v for k, v in _L3_cond_all.items() if k in ('wt', 'wg', 'w_gate', 'w_up', 'w_down', 'sw_gate', 'sw_up', 'sw_down')}
    del _L3_cond_all
    return {'x': x, 'fside_16xSxS_0': fside_16xSxS_0, 'cond_64': cond_64, 'mask_BxS_bk0': mask_BxS_bk0, 'mask_BxS_bf1': mask_BxS_bf1, 'L0_cond_g_in': _L0_cond_in['g_in'], 'L0_cond_null_attn_bias': _L0_cond_in['null_attn_bias'], 'L0_cond_Wq': _L0_cond_in['Wq'], 'L0_cond_Wkv': _L0_cond_in['Wkv'], 'L0_cond_Wo': _L0_cond_in['Wo'], 'L0_cond_g_out': _L0_cond_in['g_out'], 'L1_cond_g_norm': _L1_cond_in['g_norm'], 'L1_cond_Wq': _L1_cond_in['Wq'], 'L1_cond_Wkv': _L1_cond_in['Wkv'], 'L1_cond_q_scale': _L1_cond_in['q_scale'], 'L1_cond_k_scale': _L1_cond_in['k_scale'], 'L1_cond_null_attn_bias': _L1_cond_in['null_attn_bias'], 'L1_cond_w0': _L1_cond_in['w0'], 'L1_cond_b0': _L1_cond_in['b0'], 'L1_cond_g0': _L1_cond_in['g0'], 'L1_cond_w1': _L1_cond_in['w1'], 'L1_cond_b1': _L1_cond_in['b1'], 'L1_cond_g1': _L1_cond_in['g1'], 'L1_cond_w2': _L1_cond_in['w2'], 'L1_cond_b2': _L1_cond_in['b2'], 'L1_cond_Wout': _L1_cond_in['Wout'], 'L1_cond_g_out': _L1_cond_in['g_out'], 'L2_cond_wt': _L2_cond_in['wt'], 'L2_cond_wg': _L2_cond_in['wg'], 'L2_cond_w_gate': _L2_cond_in['w_gate'], 'L2_cond_w_up': _L2_cond_in['w_up'], 'L2_cond_w_down': _L2_cond_in['w_down'], 'L2_cond_sw_gate': _L2_cond_in['sw_gate'], 'L2_cond_sw_up': _L2_cond_in['sw_up'], 'L2_cond_sw_down': _L2_cond_in['sw_down'], 'L3_cond_wt': _L3_cond_in['wt'], 'L3_cond_wg': _L3_cond_in['wg'], 'L3_cond_w_gate': _L3_cond_in['w_gate'], 'L3_cond_w_up': _L3_cond_in['w_up'], 'L3_cond_w_down': _L3_cond_in['w_down'], 'L3_cond_sw_gate': _L3_cond_in['sw_gate'], 'L3_cond_sw_up': _L3_cond_in['sw_up'], 'L3_cond_sw_down': _L3_cond_in['sw_down']}

def reference(x, fside_16xSxS_0, cond_64, mask_BxS_bk0, mask_BxS_bf1, L0_cond_g_in, L0_cond_null_attn_bias, L0_cond_Wq, L0_cond_Wkv, L0_cond_Wo, L0_cond_g_out, L1_cond_g_norm, L1_cond_Wq, L1_cond_Wkv, L1_cond_q_scale, L1_cond_k_scale, L1_cond_null_attn_bias, L1_cond_w0, L1_cond_b0, L1_cond_g0, L1_cond_w1, L1_cond_b1, L1_cond_g1, L1_cond_w2, L1_cond_b2, L1_cond_Wout, L1_cond_g_out, L2_cond_wt, L2_cond_wg, L2_cond_w_gate, L2_cond_w_up, L2_cond_w_down, L2_cond_sw_gate, L2_cond_sw_up, L2_cond_sw_down, L3_cond_wt, L3_cond_wg, L3_cond_w_gate, L3_cond_w_up, L3_cond_w_down, L3_cond_sw_gate, L3_cond_sw_up, L3_cond_sw_down):
    import jax
    import jax.numpy as jnp

    def _L0_cond_ref(x, attn_bias, mask, g_in, null_attn_bias, null_kv, Wq, Wkv, Wo, g_out):
        import jax, jax.numpy as jnp
        import numpy as np
        B, N, DIM, H, DH = (2, 256, 128, 16, 64)
        INNER = H * DH
        EPS = 1e-05

        def layernorm(x, g):
            mean = jnp.mean(x, axis=-1, keepdims=True)
            var = jnp.var(x, axis=-1, keepdims=True)
            return (x - mean) * jax.lax.rsqrt(var + EPS) * g
        b, n, _ = x.shape
        scale = DH ** (-0.5)
        xn = layernorm(x, g_in)
        q = (xn @ Wq).reshape(b, n, H, DH).transpose(0, 2, 1, 3) * scale
        kv = xn @ Wkv
        k, v = (kv[..., :DH], kv[..., DH:])
        nk = jnp.broadcast_to(null_kv[0], (b, 1, DH))
        nv = jnp.broadcast_to(null_kv[1], (b, 1, DH))
        k = jnp.concatenate([nk, k], axis=1)
        v = jnp.concatenate([nv, v], axis=1)
        sim = jnp.einsum('bhid,bjd->bhij', q, k)
        null_col = jnp.broadcast_to(null_attn_bias[:, None, None], (H, n, 1))
        bias = jnp.concatenate([null_col, attn_bias], axis=-1)
        sim = sim + bias
        neg = -jnp.finfo(sim.dtype).max
        j = n + 1
        causal_mask = jnp.triu(jnp.ones((n, j), dtype=bool), k=j - n + 1)
        sim = jnp.where(causal_mask, neg, sim)
        mask_p = jnp.pad(mask, ((0, 0), (1, 0)), constant_values=True)
        sim = jnp.where(mask_p[:, None, None, :], sim, neg)
        attn = jax.nn.softmax(sim, axis=-1)
        out = jnp.einsum('bhij,bjd->bhid', attn, v)
        out = out.transpose(0, 2, 1, 3).reshape(b, n, INNER)
        out = out @ Wo
        return layernorm(out, g_out)

    def _L1_cond_ref(x, mask, g_norm, Wq, Wkv, q_scale, k_scale, null_kv, null_attn_bias, w0, b0, g0, w1, b1, g1, w2, b2, Wout, g_out):
        import jax, jax.numpy as jnp
        import numpy as np
        DIM = 128
        HEADS = 16
        DIM_HEAD = 64
        SCALE = 8.0

        def ln(x, g, eps=1e-05):
            mean = x.mean(axis=-1, keepdims=True)
            var = ((x - mean) ** 2).mean(axis=-1, keepdims=True)
            return (x - mean) * jax.lax.rsqrt(var + eps) * g

        def l2norm(t):
            n = jnp.maximum(jnp.linalg.norm(t, axis=-1, keepdims=True), 1e-12)
            return t / n

        def rel_pos_bias(n, w0, b0, g0, w1, b1, g1, w2, b2, dtype):
            pos = jnp.arange(-n + 1, n, dtype=dtype)[:, None]
            h = jax.nn.silu(ln(pos @ w0 + b0, g0))
            h = jax.nn.silu(ln(h @ w1 + b1, g1))
            h = h @ w2 + b2
            i = jnp.arange(n)
            idx = i[:, None] - i[None, :] + n - 1
            bias = h[idx]
            return jnp.transpose(bias, (2, 0, 1))
        b, n, _ = x.shape
        xn = ln(x, g_norm)
        q = (xn @ Wq).reshape(b, n, HEADS, DIM_HEAD).transpose(0, 2, 1, 3)
        kv = xn @ Wkv
        k, v = (kv[..., :DIM_HEAD], kv[..., DIM_HEAD:])
        nk = jnp.broadcast_to(null_kv[0], (b, 1, DIM_HEAD))
        nv = jnp.broadcast_to(null_kv[1], (b, 1, DIM_HEAD))
        k = jnp.concatenate([nk, k], axis=1)
        v = jnp.concatenate([nv, v], axis=1)
        q = l2norm(q) * q_scale
        k = l2norm(k) * k_scale
        sim = jnp.einsum('bhid,bjd->bhij', q, k) * SCALE
        bias = rel_pos_bias(n, w0, b0, g0, w1, b1, g1, w2, b2, q.dtype)
        null_bias = jnp.broadcast_to(null_attn_bias[:, None, None], (HEADS, n, 1))
        attn_bias = jnp.concatenate([null_bias, bias], axis=-1)
        sim = sim + attn_bias
        neg = -jnp.finfo(sim.dtype).max
        causal = jnp.triu(jnp.ones((n, n + 1), dtype=bool), k=2)
        sim = jnp.where(causal, neg, sim)
        m = jnp.pad(mask, ((0, 0), (1, 0)), constant_values=True)[:, None, None, :]
        sim = jnp.where(m, sim, neg)
        attn = jax.nn.softmax(sim, axis=-1)
        out = jnp.einsum('bhij,bjd->bhid', attn, v)
        out = out.transpose(0, 2, 1, 3).reshape(b, n, HEADS * DIM_HEAD)
        return ln(out @ Wout, g_out)

    def _L2_cond_ref(hidden_states, g, wt, wg, w_gate, w_up, w_down, sw_gate, sw_up, sw_down):
        import jax, jax.numpy as jnp
        import numpy as np
        B, S, H = (4, 256, 128)
        E = 8
        M = 64
        K = 2
        N_SHARED = 2
        SM = M * N_SHARED
        G = 64
        GE_TEMP = 1.0
        ALPHA = 0.001
        SEQ_AUX = True
        NORM_TOPK = True
        COS_TEMP = 0.78
        CONS_ALPHA = 0.01
        LEAKY_SLOPE = 0.01
        EPS_COS = 1e-08

        def _leaky(x):
            return jnp.where(x >= 0, x, LEAKY_SLOPE * x)

        def _moe_forward(hidden_states, g, wt, wg, w_gate, w_up, w_down, sw_gate, sw_up, sw_down):
            b, s, h = hidden_states.shape
            x = hidden_states.reshape(-1, h)
            T = x.shape[0]
            logits_h = x @ wt.T
            logits_g = g @ wg.T
            logits_g = jnp.repeat(logits_g, s, axis=0)
            logits = (logits_h + logits_g / GE_TEMP) / (1.0 + 1.0 / GE_TEMP)
            scores = jax.nn.softmax(logits, axis=-1)
            topk_w, topk_idx = jax.lax.top_k(scores, K)
            if K > 1 and NORM_TOPK:
                topk_w = topk_w / (topk_w.sum(-1, keepdims=True) + 1e-20)
            onehot = jax.nn.one_hot(topk_idx.reshape(b, s * K), E, dtype=jnp.float32)
            ce = onehot.sum(1) / (s * K / E)
            aux_loss = (ce * scores.reshape(b, s, E).mean(1)).sum(1).mean() * ALPHA
            gp = _leaky(jnp.einsum('th,ehm->etm', x, w_gate))
            up = jnp.einsum('th,ehm->etm', x, w_up)
            y_all = jnp.einsum('etm,emh->eth', gp * up, w_down)
            y_sel = y_all[topk_idx, jnp.arange(T)[:, None], :]
            y = (y_sel * topk_w[..., None]).sum(1).reshape(b, s, h)
            p = _leaky(hidden_states @ sw_gate) * (hidden_states @ sw_up) @ sw_down
            y = y + p
            num = jnp.sum(y * p, -1)
            den = jnp.maximum(jnp.linalg.norm(y, axis=-1), EPS_COS) * jnp.maximum(jnp.linalg.norm(p, axis=-1), EPS_COS)
            closs = CONS_ALPHA * jnp.mean(num / den / (1.0 + COS_TEMP))
            return (y, aux_loss + closs)
        y, _ = _moe_forward(hidden_states, g, wt, wg, w_gate, w_up, w_down, sw_gate, sw_up, sw_down)
        return y

    def _L3_cond_ref(hidden_states, g, wt, wg, w_gate, w_up, w_down, sw_gate, sw_up, sw_down):
        import jax, jax.numpy as jnp
        import numpy as np
        B, S, H = (4, 256, 128)
        E = 8
        M = 64
        K = 2
        N_SHARED = 2
        SM = M * N_SHARED
        G = 64
        GE_TEMP = 1.0
        ALPHA = 0.001
        SEQ_AUX = True
        NORM_TOPK = True
        COS_TEMP = 0.78
        CONS_ALPHA = 0.01
        LEAKY_SLOPE = 0.01
        EPS_COS = 1e-08

        def _leaky(x):
            return jnp.where(x >= 0, x, LEAKY_SLOPE * x)

        def _moe_forward(hidden_states, g, wt, wg, w_gate, w_up, w_down, sw_gate, sw_up, sw_down):
            b, s, h = hidden_states.shape
            x = hidden_states.reshape(-1, h)
            T = x.shape[0]
            logits_h = x @ wt.T
            logits_g = g @ wg.T
            logits_g = jnp.repeat(logits_g, s, axis=0)
            logits = (logits_h + logits_g / GE_TEMP) / (1.0 + 1.0 / GE_TEMP)
            scores = jax.nn.softmax(logits, axis=-1)
            topk_w, topk_idx = jax.lax.top_k(scores, K)
            if K > 1 and NORM_TOPK:
                topk_w = topk_w / (topk_w.sum(-1, keepdims=True) + 1e-20)
            onehot = jax.nn.one_hot(topk_idx.reshape(b, s * K), E, dtype=jnp.float32)
            ce = onehot.sum(1) / (s * K / E)
            aux_loss = (ce * scores.reshape(b, s, E).mean(1)).sum(1).mean() * ALPHA
            gp = _leaky(jnp.einsum('th,ehm->etm', x, w_gate))
            up = jnp.einsum('th,ehm->etm', x, w_up)
            y_all = jnp.einsum('etm,emh->eth', gp * up, w_down)
            y_sel = y_all[topk_idx, jnp.arange(T)[:, None], :]
            y = (y_sel * topk_w[..., None]).sum(1).reshape(b, s, h)
            p = _leaky(hidden_states @ sw_gate) * (hidden_states @ sw_up) @ sw_down
            y = y + p
            num = jnp.sum(y * p, -1)
            den = jnp.maximum(jnp.linalg.norm(y, axis=-1), EPS_COS) * jnp.maximum(jnp.linalg.norm(p, axis=-1), EPS_COS)
            closs = CONS_ALPHA * jnp.mean(num / den / (1.0 + COS_TEMP))
            return (y, aux_loss + closs)
        y, _ = _moe_forward(hidden_states, g, wt, wg, w_gate, w_up, w_down, sw_gate, sw_up, sw_down)
        return y
    x = x + _L0_cond_ref(x, fside_16xSxS_0, mask_BxS_bk0, L0_cond_g_in, L0_cond_null_attn_bias, cond_64, L0_cond_Wq, L0_cond_Wkv, L0_cond_Wo, L0_cond_g_out)
    x = x + _L1_cond_ref(x, mask_BxS_bf1, L1_cond_g_norm, L1_cond_Wq, L1_cond_Wkv, L1_cond_q_scale, L1_cond_k_scale, cond_64, L1_cond_null_attn_bias, L1_cond_w0, L1_cond_b0, L1_cond_g0, L1_cond_w1, L1_cond_b1, L1_cond_g1, L1_cond_w2, L1_cond_b2, L1_cond_Wout, L1_cond_g_out)
    x = x + _L2_cond_ref(x, cond_64, L2_cond_wt, L2_cond_wg, L2_cond_w_gate, L2_cond_w_up, L2_cond_w_down, L2_cond_sw_gate, L2_cond_sw_up, L2_cond_sw_down)
    x = x + _L3_cond_ref(x, cond_64, L3_cond_wt, L3_cond_wg, L3_cond_w_gate, L3_cond_w_up, L3_cond_w_down, L3_cond_sw_gate, L3_cond_sw_up, L3_cond_sw_down)
    return x

_drawn_inputs = setup_inputs


def setup_inputs(seed=0):
    import zlib

    import numpy as np

    out = dict(_drawn_inputs(seed))
    spreads = {'L0_cond_g_in': (1.0, 0.2),
     'L0_cond_g_out': (1.0, 0.2),
     'L1_cond_g_norm': (1.0, 0.2),
     'L1_cond_q_scale': (1.0, 0.2),
     'L1_cond_k_scale': (1.0, 0.2),
     'L1_cond_b0': (0.0, 0.36),
     'L1_cond_g0': (1.0, 0.6),
     'L1_cond_b1': (0.0, 0.27),
     'L1_cond_g1': (1.0, 0.6),
     'L1_cond_b2': (0.0, 0.416),
     'L1_cond_g_out': (1.0, 0.2)}
    factors = {}
    for name, (base, spread) in spreads.items():
        noise = np.random.default_rng([zlib.crc32(name.encode()), seed]).standard_normal(out[name].shape)
        drawn = base * np.exp(spread * noise) if base else spread * noise
        out[name] = jnp.asarray(drawn.astype(out[name].dtype))
    for name, factor in factors.items():
        out[name] = (out[name] * factor).astype(out[name].dtype)
    return out
```

```python
from contextlib import ExitStack

import numpy as np

import concourse.bass as bass
from concourse import mybir

F32 = mybir.dt.float32
F32R = mybir.dt.float32r
U8 = mybir.dt.uint8
ALU = mybir.AluOpType
ACT = mybir.ActivationFunctionType
AX = mybir.AxisListType

P = 128
B, N, D = 4, 256, 128
H, DH = 16, 64
INNER = H * DH
TILES = B * N // P
COLS = (P + 2, 2 * P + 2)
E, M, SM, G = 8, 64, 128, 64
EPS = 1e-5
FAR = 1e30
HEADS = 2 * H
HALF_T = 512
EXPERT_TILES = E * M // P
DOWN_TILES = EXPERT_TILES + 1


def attention_order():
    quads = [(0, 4 * g, 4) for g in range(4)] + [(1, H + 2 * g, 2) for g in range(8)]
    order = []
    for i in range(HEADS + 12):
        if i < HEADS:
            order.append(("S", i))
        for n, (half, first, k) in enumerate(quads):
            last = first + k - 1
            if last == i - 3:
                order.append(("T", n))
            if last == i - 5:
                order.append(("V", n))
        for half, last in ((0, H - 1), (1, HEADS - 1)):
            if i == last + 4:
                order.append(("Z", half))
            if i == last + 6:
                order.append(("Y", half))
            if i == last + 8:
                order += [("X", 2 * half), ("X", 2 * half + 1)]
            if i == last + 10:
                order.append(("W", half))
    return quads, order


QUADS, ORDER = attention_order()


def transpose_uses():
    uses = {}
    for half in range(2):
        uses["xn", half] = len(uses)
    for half in range(2):
        uses["k", half] = len(uses)
        for g in range(4):
            uses["q", half, g] = len(uses)
    for kind, n in ORDER:
        if kind in "TZX":
            uses[kind, n] = len(uses)
    return uses


USE = transpose_uses()
USES = len(USE)
assert USES % 2 == 0
PROJ = {("q", 0, 0): 0, ("q", 0, 1): 1, ("q", 1, 0): 2, ("q", 1, 1): 3, ("out", 0): 4, ("out", 1): 5}
PROJS = len(PROJ)


class Chain:

    def __init__(self, eng, sem):
        self.eng, self.sem, self.base, self.n = eng, sem, 0, 0

    def __call__(self, instruction):
        instruction.then_inc(self.sem, 1)
        self.n += 1
        return instruction

    def settle(self):
        self.eng.wait_ge(self.sem, self.base + self.n)

    def enter(self, iteration, per_iteration):
        self.before, self.per = self.base + self.n, per_iteration
        self.base, self.n = self.before + iteration * per_iteration, 0

    def leave(self, iterations):
        assert self.n == self.per, (self.n, self.per)
        self.base, self.n = self.before + iterations * self.per, 0


def build(nc, a, out):
    with ExitStack() as ctx:
        _build(nc, ctx, a, out)


def _build(nc, ctx, a, out):
    def sb(name, shape, dt=F32):
        return ctx.enter_context(nc.sbuf_tensor("sb_" + name, shape, dt))

    def sem(name):
        return ctx.enter_context(nc.semaphore(name))

    bank = [ctx.enter_context(nc.psum_tensor(f"bank{i}", [P, 512], F32)) for i in range(8)]
    s_bank, t_bank, o_bank, p_bank = bank[0:2], bank[2:4], bank[4:6], bank[6:8]

    ident = sb("ident", [P, P])
    x_sb = sb("x", [P, TILES, D])
    with ExitStack() as first:
        bias0 = first.enter_context(nc.sbuf_tensor("sb_bias0", [P, H, P], F32))
        bias1 = first.enter_context(nc.sbuf_tensor("sb_bias1", [P, H, N], F32))
    moe = Moe(sb, sem, bank, ident, x_sb)
    sb("rest_of_bias", [P, H * (P + N) - Moe.WEIGHT_WORDS])
    attention = ctx.enter_context(ExitStack())
    permanent = sb

    def sb(name, shape, dt=F32):
        return attention.enter_context(nc.sbuf_tensor("sb_" + name, shape, dt))

    wqkv = sb("wqkv", [P, INNER + P])
    w_hi = [sb(f"w_hi{i}", [P, INNER + P], F32R) for i in range(2)]
    w_lo = [sb(f"w_lo{i}", [P, INNER + P], F32R) for i in range(2)]
    wo = [sb(f"wo{i}", [P, H // 2, D]) for i in range(2)]
    gain_in = sb("gain_in", [P, 2])
    gain_out = sb("gain_out", [P, 2, D])
    qk_scale = sb("qk_scale", [P, 2, DH])
    k_gain = sb("k_gain", [P, DH])
    null_kv = sb("null_kv", [2, DH])
    null_sq = sb("null_sq", [2, DH])
    null_split = sb("null_split", [2, 4, DH], F32R)
    null_s = sb("null_s", [2, 4])
    null_v = sb("null_v", [H, H, DH])
    null_bias = sb("null_bias", [P, 2, H])
    mask_u8 = sb("mask_u8", [P, 2, B, N], U8)
    mask = sb("mask", [P, 2, B, N])
    toep = sb("toep", [P, H, N])
    nb = [sb("nb0", [P, H, COLS[0]]), sb("nb1", [P, H, COLS[1]])]
    minus_half = sb("minus_half", [P, 2 * H + 2])
    stats = sb("stats", [P, 6])
    mv = sb("mv", [P, 2, 2])
    var_e = sb("var_e", [P, 2])
    rstd = sb("rstd", [P, 2])
    xn = sb("xn", [P, 2, D])
    xnT_hi = sb("xnT_hi", [P, 2, P], F32R)
    xnT_lo = sb("xnT_lo", [P, 2, P], F32R)
    sq = sb("sq", [P, INNER + DH])
    ss = sb("ss", [P, 2, H + 1])
    rq = sb("rq", [P, 2, H + 1])
    qn = sb("qn", [P, H, DH])
    q_split = sb("q_split", [P, H, 2, DH], F32R)
    kn = sb("kn", [P, DH])
    k_split = sb("k_split", [P, 4, DH], F32R)
    qT = sb("qT", [P, 2, H, P], F32R)
    k_hi = sb("k_hi", [P, COLS[1]], F32R)
    k_lo = sb("k_lo", [P, COLS[1]], F32R)
    v_sb = sb("v", [P, 2, DH])
    t_sb = sb("t", [P, 4, COLS[1]])
    low = sb("low", [P, HEADS])
    total = sb("total", [P, HEADS])
    recip = sb("recip", [P, HEADS])
    prob = [sb("prob0", [P, H, COLS[0]]), sb("prob1", [P, H, COLS[1]])]
    pT = sb("pT", [P, 2, 4, P])
    nullT = sb("nullT", [H, P])
    o_sb = sb("o", [P, INNER])
    oT = sb("oT", [P, H // 2, P])
    ln_sb = sb("ln", [P, 2, D])
    pos_rows = sb("pos_rows", [2, N])
    w0b0 = sb("w0b0", [2, D])
    mlp_rows = sb("mlp_rows", [P, 3, D])
    w1 = sb("w1", [D, D])
    w2 = sb("w2", [D, H])
    b2 = sb("b2", [H, 1])
    mh = sb("mh", [P, 2, D])
    me = sb("me", [P, 2, D])
    mhT = sb("mhT", [P, N])
    table = sb("table", [H, N + P])
    scratch = nc.dram_tensor("bias_table", [H, P, N + P], F32, kind="Internal").ap()

    loaded = {n: sem("loaded_" + n) for n in ("start", "mlp", "wqkv0", "wqkv1", "attn", "bias0", "bias1", "moe")}
    dve_step, act_step, pool_step = sem("dve_step"), sem("act_step"), sem("pool_step")
    w_staged = sem("w_staged")
    consts_ready = sem("consts_ready")
    mlp_pe, mlp_dve, mlp_act, mlp_pool = sem("mlp_pe"), sem("mlp_dve"), sem("mlp_act"), sem("mlp_pool")
    table_stored, toep_loaded, bias_cut = sem("table_stored"), sem("toep_loaded"), sem("bias_cut")
    null_ready, null_T, null_placed = sem("null_ready"), sem("null_T"), sem("null_placed")
    nb_edges = sem("nb_edges")
    stats_ready, rstd_ready = sem("stats_ready"), sem("rstd_ready")
    xn_ready, xnT_ready = sem("xn_ready"), sem("xnT_ready")
    t_ready = sem("t_ready")
    t_free = [sem("t_free0"), sem("t_free1")]
    p_ready = sem("p_ready")
    p_free = [sem("p_free0"), sem("p_free1")]
    hi_done = sem("hi_done")
    sq_done, norms_ready, rq_ready = sem("sq_done"), sem("norms_ready"), sem("rq_ready")
    qn_ready, q_split_ready, k_split_ready = sem("qn_ready"), sem("q_split_ready"), sem("k_split_ready")
    kv_proj, kv_ready = sem("kv_proj"), sem("kv_ready")
    s_ready, masked, probs = sem("s_ready"), sem("masked"), sem("probs")
    nb_ready = sem("nb_ready")
    pT_ready, v_done = sem("pT_ready"), sem("v_done")
    nullT_ready, o_done, o_ready, oT_ready = sem("nullT_ready"), sem("o_done"), sem("o_ready"), sem("oT_ready")
    out_stats, out_rstd, tile_done = sem("out_stats"), sem("out_rstd"), sem("tile_done")
    stored = sem("stored")
    passed = sem("passed")

    attention.close()
    moe.allocate(permanent)

    def wait_apart(eng, waits):
        for which, value in waits:
            eng.wait_ge(which, value)
        eng.sem_inc(passed, 1)

    block = ctx.enter_context(nc.Block())

    CONSTS = 6

    @block.sync
    def _(sp):
        for given_back in (*t_free, *p_free, v_done, probs, o_ready, moe.hidden, moe.added):
            sp.sem_inc(given_back, CREDIT)
        sp.dma_start(x_sb[:], a["x"].rearrange("(t p) d -> p t d", p=P)).then_inc(loaded["start"], 16)
        sp.dma_start(ident[:], a["ident"]).then_inc(loaded["start"], 16)
        sp.dma_start(mask_u8[:, 0], a["mask0"].partition_broadcast(P)).then_inc(loaded["start"], 16)
        sp.dma_start(mask_u8[:, 1], a["mask1"].partition_broadcast(P)).then_inc(loaded["start"], 16)
        sp.dma_start(wqkv[:, 0:INNER], a["L0_cond_Wq"]).then_inc(loaded["wqkv0"], 16)
        sp.dma_start(wqkv[:, INNER:], a["L0_cond_Wkv"]).then_inc(loaded["wqkv0"], 16)
        sp.dma_start(bias0[:], a["bias"][:, 0:P, 0:P].rearrange("h q k -> q h k")).then_inc(loaded["bias0"], 16)
        sp.dma_start(bias1[:], a["bias"][:, P:N, :].rearrange("h q k -> q h k")).then_inc(loaded["bias1"], 16)
        sp.wait_ge(w_staged, 1)
        sp.dma_start(wqkv[:, 0:INNER], a["L1_cond_Wq"]).then_inc(loaded["wqkv1"], 16)
        sp.dma_start(wqkv[:, INNER:], a["L1_cond_Wkv"]).then_inc(loaded["wqkv1"], 16)
        sp.wait_ge(mlp_dve, MLP_DVE_TABLE)
        sp.dma_start(scratch, table[:].unsqueeze(1).to_broadcast([H, P, N + P])).then_inc(table_stored, 16)
        sp.wait_ge(table_stored, 16)
        sp.dma_start(toep[:], bass.AP(tensor=scratch.tensor, offset=P - 1,
                                      ap=[[N + P - 1, P], [P * (N + P), H], [1, N]])).then_inc(toep_loaded, 16)
        sp.wait_ge(nb_ready, B * 8)
        moe.load(sp, a)
        moe.store(sp, out, stored)

    @block.scalar
    def _(act):
        act.dma_start(pos_rows[:], a["pos_rows"]).then_inc(loaded["mlp"], 16)
        act.dma_start(w0b0[0:1, :], a["L1_cond_w0"]).then_inc(loaded["mlp"], 16)
        act.dma_start(w0b0[1:2, :], a["L1_cond_b0"].rearrange("(o d) -> o d", o=1)).then_inc(loaded["mlp"], 16)
        for n, name in enumerate(("g0", "g1", "b1")):
            act.dma_start(mlp_rows[:, n], a["L1_cond_" + name].partition_broadcast(P)).then_inc(loaded["mlp"], 16)
        act.dma_start(w1[:], a["L1_cond_w1"]).then_inc(loaded["mlp"], 16)
        act.dma_start(w2[:], a["L1_cond_w2"]).then_inc(loaded["mlp"], 16)
        act.dma_start(b2[:], a["L1_cond_b2"].rearrange("(h o) -> h o", o=1)).then_inc(loaded["mlp"], 16)
        loads = [
            (gain_in[:, 0:1], a["L0_cond_g_in"].rearrange("(d o) -> d o", o=1)),
            (gain_in[:, 1:2], a["L1_cond_g_norm"].rearrange("(d o) -> d o", o=1)),
            (gain_out[:, 0], a["L0_cond_g_out"].partition_broadcast(P)),
            (gain_out[:, 1], a["L1_cond_g_out"].partition_broadcast(P)),
            (qk_scale[:, 0], a["L1_cond_q_scale"].partition_broadcast(P)),
            (qk_scale[:, 1], a["L1_cond_k_scale"].partition_broadcast(P)),
            (null_bias[:, 0], a["L0_cond_null_attn_bias"].partition_broadcast(P)),
            (null_bias[:, 1], a["L1_cond_null_attn_bias"].partition_broadcast(P)),
            (null_kv[:], a["null_key_rows"]),
            (null_v[:].rearrange("h a d -> h (a d)"), a["null_v_blocks"]),
            (wo[0][:], a["L0_cond_Wo"].rearrange("(j p) d -> p j d", p=P)),
            (wo[1][:], a["L1_cond_Wout"].rearrange("(j p) d -> p j d", p=P)),
        ]
        assert len(loads) == ATTN_LOADS
        for dst, src in loads:
            act.dma_start(dst, src).then_inc(loaded["attn"], 16)
        for layer in range(2):
            act.wait_ge(mlp_dve, MLP_DVE_H[layer])
            act.activation(me[:], mh[:], ACT.Exp, scale=-1.0).then_inc(mlp_act, 1)
        chain = Chain(act, act_step)
        for layer in range(2):
            act.wait_ge(null_T, layer + 1)
            act.activation(k_hi[:, 0:2], o_bank[0][:, 0:2], ACT.Copy).then_inc(null_placed, 1)
            act.activation(k_lo[:, 0:2], o_bank[0][:, 2:4], ACT.Copy).then_inc(null_placed, 1)
            with act.Fori(layer * B, layer * B + B) as s:
                chain.enter(s - layer * B, ACT_CHAIN[layer])
                for half in range(2):
                    n = USE["xn", half]
                    act.wait_ge(t_ready, s * USES + n + 1)
                    act.activation(xnT_hi[:, half], t_bank[n % 2][:, 0:P], ACT.Copy).then_inc(hi_done, 1)
                for half in range(2):
                    for c in range(2):
                        n = PROJ["q", half, c]
                        cols = slice(c * 8, c * 8 + 8)
                        src = p_bank[n % 2][:].rearrange("p (h d) -> p h d", d=DH)
                        if layer == 0:
                            act.wait_ge(p_ready, s * PROJS + n + 1)
                            if half == 1:
                                act.wait_ge(t_ready, s * USES + USE["q", 0, 2 * c + 1] + 1)
                            act.activation(q_split[:, cols, 0], src, ACT.Copy).then_inc(hi_done, 1)
                        else:
                            act.wait_ge(p_ready, s * PROJS + n + 1)
                            if half == 1:
                                act.wait_ge(norms_ready, (s - B) * 2 + 1)
                            act.activation(sq[:, c * 512:c * 512 + 512], p_bank[n % 2][:], ACT.Square)\
                                .then_inc(sq_done, 1)
                    act.wait_ge(kv_proj, s * 2 + half + 1)
                    if layer == 1:
                        act.activation(sq[:, INNER:], s_bank[half][:, 0:DH], ACT.Square).then_inc(sq_done, 1)
                    act.activation(v_sb[:, half], s_bank[half][:, DH:P], ACT.Copy).then_inc(kv_ready, 1)
                    act.wait_ge(qn_ready, s * 2 + half + 1)
                    if half == 1:
                        act.wait_ge(t_ready, s * USES + USE["k", 0] + 1)
                    act.activation(k_split[:, 0:2], kn[:].unsqueeze(1).to_broadcast([P, 2, DH]), ACT.Copy)\
                        .then_inc(hi_done, 1)
                    if layer == 1:
                        if half == 1:
                            act.wait_ge(t_ready, s * USES + USE["q", 0, 3] + 1)
                        act.activation(q_split[:, :, 0], qn[:], ACT.Copy).then_inc(hi_done, 1)
                    n = USE["k", half]
                    act.wait_ge(t_ready, s * USES + n + 1)
                    at = slice(2 + half * P, 2 + half * P + P)
                    act.activation(k_hi[:, at], t_bank[n % 2][:, 0:P], ACT.Copy).then_inc(kv_ready, 1)
                    act.activation(k_lo[:, at], t_bank[n % 2][:, P:2 * P], ACT.Copy).then_inc(t_free[n % 2], 1)
                    for g in range(0, 4, 2):
                        n = USE["q", half, g]
                        act.wait_ge(t_ready, s * USES + n + 1)
                        act.activation(qT[:, half, 4 * g:4 * g + 4].rearrange("p h q -> p (h q)"),
                                       t_bank[n % 2][:], ACT.Copy).then_inc(t_free[n % 2], 1)
                for kind, n in ORDER:
                    if kind == "S":
                        half, h = divmod(n, H)
                        act.wait_ge(masked, s * HEADS + HEADS + n + 1)
                        act.activation(prob[half][:, h], t_sb[:, n % 4, 0:COLS[half]], ACT.Exp, scale=-1.0,
                                       bias=low[:, n:n + 1], accum_out=total[:, n:n + 1]).then_inc(probs, 1)
                    if kind == "Z":
                        u = USE["Z", n]
                        act.wait_ge(t_ready, s * USES + u + 1)
                        act.activation(nullT[:], t_bank[u % 2][0:H, 0:P], ACT.Copy).then_inc(t_free[u % 2], 1)
                    if kind == "X":
                        u = USE["X", n]
                        act.wait_ge(t_ready, s * USES + u + 1)
                        act.activation(oT[:, 4 * (n % 2):4 * (n % 2) + 4].rearrange("p h q -> p (h q)"),
                                       t_bank[u % 2][:], ACT.Copy).then_inc(t_free[u % 2], 1)
            chain.leave(B)
        moe.scalar(act)

    @block.gpsimd
    def _(pool):
        fill = -FAR
        pool.wait_ge(loaded["bias0"], 16)
        pool.affine_select(out=bias0[:], in_=bias0[:], compare_op=ALU.is_ge, fill=fill, base=0,
                           pattern=[[0, H], [-1, P]], channel_multiplier=1).then_inc(bias_cut, 1)
        pool.wait_ge(loaded["bias1"], 16)
        pool.affine_select(out=bias1[:, :, P:N], in_=bias1[:, :, P:N], compare_op=ALU.is_ge, fill=fill, base=0,
                           pattern=[[0, H], [-1, P]], channel_multiplier=1).then_inc(bias_cut, 1)
        pool.wait_ge(bias_cut, 2)
        pool.wait_ge(consts_ready, CONSTS)
        for layer in range(2):
            pool.wait_ge(mlp_dve, MLP_DVE_VAR[layer])
            pool.tensor_tensor(rstd[:], var_e[:], minus_half[:, 0:2], ALU.pow).then_inc(mlp_pool, 1)
        pool.wait_ge(null_ready, 1)
        pool.tensor_tensor(null_s[:, 1:2], null_s[:, 0:1], minus_half[0:2, 0:1], ALU.pow).then_inc(mlp_pool, 1)
        for layer in range(2):
            if layer == 1:
                pool.wait_ge(toep_loaded, 16)
            src = ((bias0, slice(0, P)), (bias1, slice(0, N))) if layer == 0 else \
                ((toep, slice(P, N)), (toep, slice(0, N)))
            with pool.Fori(layer * B, layer * B + B) as s:
                b = s - layer * B
                pool.wait_ge(stats_ready, s + 1)
                pool.tensor_tensor(rstd[:], var_e[:], minus_half[:, 0:2], ALU.pow).then_inc(rstd_ready, 1)

                def cut(half, g):
                    wait_apart(pool, [(masked, s * HEADS + half * H + 4 * g + 4)])
                    tile, cols = src[half]
                    hs = slice(4 * g, 4 * g + 4)
                    keys = COLS[half] - 2
                    pool.tensor_tensor(
                        nb[half][:, hs, 2:],
                        mask[:, layer, bass.ds(b, 1), 0:keys].to_broadcast([P, 4, keys]),
                        tile[:, hs, cols], ALU.subtract).then_inc(nb_ready, 1)

                cut(0, 0)
                cut(0, 1)
                if layer == 1:
                    for half in range(2):
                        pool.wait_ge(norms_ready, (s - B) * 2 + half + 1)
                        pool.tensor_tensor(rq[:, half], ss[:, half], minus_half[:, 0:H + 1], ALU.pow)\
                            .then_inc(rq_ready, 1)
                cut(0, 2)
                cut(0, 3)
                for g in range(4):
                    cut(1, g)
                for half in range(2):
                    pool.wait_ge(out_stats, s * 2 + half + 1)
                    pool.tensor_tensor(rstd[:, half:half + 1], var_e[:, half:half + 1], minus_half[:, 0:1],
                                       ALU.pow).then_inc(out_rstd, 1)
        moe.gpsimd(pool)

    @block.vector
    def _(dve):
        chain = Chain(dve, dve_step)
        dve.memset(minus_half[:], -0.5).then_inc(consts_ready, 1)
        dve.memset(table[:], -FAR).then_inc(masked, HEADS)
        dve.memset(nb[0][:], FAR).then_inc(consts_ready, 1)
        dve.memset(nb[1][:], FAR).then_inc(consts_ready, 1)
        dve.wait_ge(loaded["start"], 64)
        for layer in range(2):
            dve.tensor_scalar(mask[:, layer], mask_u8[:, layer], -FAR, FAR, ALU.mult, ALU.add)\
                .then_inc(consts_ready, 1)
        dve.wait_ge(loaded["attn"], 16 * ATTN_LOADS)
        chain(dve.tensor_tensor(k_gain[:], qk_scale[:, 0], qk_scale[:, 1], ALU.mult))
        chain.settle()
        dve.tensor_scalar(k_gain[:], k_gain[:], -8.0, None, ALU.mult).then_inc(consts_ready, 1)
        chain(dve.tensor_tensor(null_sq[:], null_kv[:], null_kv[:], ALU.mult))
        chain.settle()
        chain(dve.tensor_reduce(null_s[:, 0:1], null_sq[:], AX.X, ALU.add))
        chain.settle()
        dve.tensor_scalar(null_s[:, 0:1], null_s[:, 0:1], 1e-24, None, ALU.max).then_inc(null_ready, 1)

        def split_weights(layer):
            dve.wait_ge(loaded[f"wqkv{layer}"], 32)
            chain(dve.tensor_scalar(wqkv[:], wqkv[:], gain_in[:, layer:layer + 1], None, ALU.mult))
            chain.settle()
            chain(dve.tensor_copy(w_hi[layer][:], wqkv[:]))
            chain.settle()
            dve.tensor_tensor(w_lo[layer][:], wqkv[:], w_hi[layer][:].bitcast(F32), ALU.subtract)\
                .then_inc(w_staged, 1)

        def layer_norm_stats(src, half, signal):
            chain(dve.bn_stats(stats[:], src))
            wait_apart(dve, [(dve_step, chain.base + chain.n)])
            chain(dve.bn_aggr(mv[:, half], stats[:]))
            chain.settle()
            dve.tensor_scalar(var_e[:, half:half + 1], mv[:, half, 1:2], EPS, None, ALU.add).then_inc(signal, 1)

        split_weights(0)
        psum_h = [bank[2 + n][:, 0:D] for n in range(2)]
        for layer in range(2):
            dve.wait_ge(mlp_pe, MLP_PE_H[layer])
            if layer == 1:
                dve.wait_ge(loaded["mlp"], 16 * 9)
                for n in range(2):
                    chain(dve.tensor_tensor(mh[:, n], psum_h[n], mlp_rows[:, 2], ALU.add))
                chain.settle()
            for n in range(2):
                layer_norm_stats(psum_h[n] if layer == 0 else mh[:, n], n, mlp_dve)
            dve.wait_ge(mlp_pool, layer + 1)
            if layer == 0:
                dve.wait_ge(loaded["mlp"], 16 * 9)
            for n in range(2):
                chain(dve.tensor_scalar(mh[:, n], psum_h[n] if layer == 0 else mh[:, n], mv[:, n, 0:1],
                                        rstd[:, n:n + 1], ALU.subtract, ALU.mult))
            chain.settle()
            dve.tensor_tensor(mh[:], mh[:], mlp_rows[:, layer].unsqueeze(1).to_broadcast([P, 2, D]), ALU.mult)\
                .then_inc(mlp_dve, 1)
            dve.wait_ge(mlp_act, layer + 1)
            chain(dve.tensor_scalar(me[:], me[:], 1.0, None, ALU.add))
            chain.settle()
            chain(dve.reciprocal(me[:], me[:]))
            chain.settle()
            dve.tensor_tensor(mh[:], mh[:], me[:], ALU.mult).then_inc(mlp_dve, 1)
            dve.wait_ge(mlp_pe, MLP_PE_T[layer])
            dve.tensor_copy(mhT[:], bank[4][:, 0:N]).then_inc(mlp_dve, 1)
        dve.wait_ge(mlp_pe, MLP_PE_TABLE)
        dve.wait_ge(masked, HEADS)
        dve.tensor_scalar(table[:, 0:N], bank[5][0:H, 0:N], b2[:], None, ALU.add).then_inc(mlp_dve, 1)
        split_weights(1)

        for layer in range(2):
            dve.wait_ge(consts_ready, CONSTS)
            dve.wait_ge(masked, (layer * B + 1) * HEADS)
            for half in range(2):
                chain(dve.tensor_scalar(nb[half][:, :, 0], null_bias[:, layer], -1.0, None, ALU.mult))
            if layer == 0:
                chain(dve.tensor_scalar(null_sq[:], null_kv[:], -0.125, None, ALU.mult))
            else:
                dve.wait_ge(mlp_pool, 3)
                chain(dve.scalar_tensor_tensor(null_sq[:], null_kv[:], null_s[:, 1:2], k_gain[0:2], ALU.mult,
                                               ALU.mult))
            chain.settle()
            twice = null_sq[:].unsqueeze(1).to_broadcast([2, 2, DH])
            if layer == 1:
                dve.wait_ge(null_T, 1)
            chain(dve.tensor_copy(null_split[:, 0:2], twice))
            chain.settle()
            dve.tensor_tensor(null_split[:, 2:4], twice, null_split[:, 0:2].bitcast(F32), ALU.subtract)\
                .then_inc(null_ready, 1)
            if layer == 0:
                dve.wait_ge(loaded["start"], 64)
            with dve.Fori(layer * B, layer * B + B) as s:
                chain.enter(s - layer * B, DVE_CHAIN[layer])
                tile0 = (s - layer * B) * 2
                for half in range(2):
                    x_t = x_sb[:, bass.ds(tile0 + half, 1), :].rearrange("p a d -> p (a d)")
                    chain(dve.bn_stats(stats[:], x_t))
                    wait_apart(dve, [(dve_step, chain.base + chain.n)])
                    chain(dve.bn_aggr(mv[:, half], stats[:]))
                    chain.settle()
                dve.tensor_scalar(var_e[:], mv[:, :, 1], EPS, None, ALU.add).then_inc(stats_ready, 1)
                dve.wait_ge(rstd_ready, s + 1)
                for half in range(2):
                    x_t = x_sb[:, bass.ds(tile0 + half, 1), :].rearrange("p a d -> p (a d)")
                    dve.tensor_scalar(xn[:, half], x_t, mv[:, half, 0:1], rstd[:, half:half + 1],
                                      ALU.subtract, ALU.mult).then_inc(xn_ready, 1)
                for half in range(2):
                    n = USE["xn", half]
                    dve.wait_ge(hi_done, (s * HI[0] if layer == 0 else s_hi(s, 1)) + half + 1)
                    dve.tensor_tensor(xnT_lo[:, half], t_bank[n % 2][:, 0:P], xnT_hi[:, half].bitcast(F32),
                                      ALU.subtract).then_inc(t_free[n % 2], 1)
                for half in range(2):
                    if layer == 0:
                        for c in range(2):
                            n = PROJ["q", half, c]
                            dve.wait_ge(hi_done, s * HI[0] + 2 + half * 3 + c + 1)
                            hs = slice(c * 8, c * 8 + 8)
                            dve.tensor_tensor(q_split[:, hs, 1], p_bank[n % 2][:].rearrange("p (h d) -> p h d", d=DH),
                                              q_split[:, hs, 0].bitcast(F32), ALU.subtract).then_inc(p_free[n % 2], 1)
                        dve.wait_ge(kv_ready, s * 4 + half * 2 + 1)
                        dve.tensor_scalar(kn[:], s_bank[half][:, 0:DH], -0.125, None, ALU.mult)\
                            .then_inc(qn_ready, 1)
                    else:
                        dve.wait_ge(sq_done, (s - B) * 6 + half * 3 + 3)
                        chain(dve.tensor_reduce(ss[:, half], sq[:].rearrange("p (h d) -> p h d", d=DH), AX.X, ALU.add))
                        chain.settle()
                        dve.tensor_scalar(ss[:, half], ss[:, half], 1e-24, None, ALU.max).then_inc(norms_ready, 1)
                        dve.wait_ge(rq_ready, (s - B) * 2 + half + 1)
                        if half == 1:
                            dve.wait_ge(hi_done, s_hi(s, 1) + 4)
                            dve.wait_ge(q_split_ready, (s - B) * 2 + 1)
                        for c in range(2):
                            n = PROJ["q", half, c]
                            hs = slice(c * 8, c * 8 + 8)
                            dve.tensor_tensor(qn[:, hs], p_bank[n % 2][:].rearrange("p (h d) -> p h d", d=DH),
                                              rq[:, half, hs].unsqueeze(2).to_broadcast([P, 8, DH]), ALU.mult)\
                                .then_inc(p_free[n % 2], 1)
                        dve.wait_ge(kv_ready, s * 4 + half * 2 + 1)
                        dve.scalar_tensor_tensor(kn[:], s_bank[half][:, 0:DH], rq[:, half, H:H + 1],
                                                 k_gain[:], ALU.mult, ALU.mult).then_inc(qn_ready, 1)
                    base = s * HI[0] + 2 + half * 3 + 3 if layer == 0 else s_hi(s, 1) + 2 + half * 2 + 1
                    dve.wait_ge(hi_done, base)
                    dve.tensor_tensor(k_split[:, 2:4], kn[:].unsqueeze(1).to_broadcast([P, 2, DH]),
                                      k_split[:, 0:2].bitcast(F32), ALU.subtract).then_inc(k_split_ready, 1)
                    if layer == 1:
                        dve.wait_ge(hi_done, base + 1)
                        dve.tensor_tensor(q_split[:, :, 1], qn[:], q_split[:, :, 0].bitcast(F32), ALU.subtract)\
                            .then_inc(q_split_ready, 1)
                    for g in range(1, 4, 2):
                        n = USE["q", half, g]
                        dve.wait_ge(t_ready, s * USES + n + 1)
                        dve.tensor_copy(qT[:, half, 4 * g:4 * g + 4].rearrange("p h q -> p (h q)"),
                                        t_bank[n % 2][:]).then_inc(t_free[n % 2], 1)
                for kind, n in ORDER:
                    if kind == "S":
                        half, h = divmod(n, H)
                        waits = [(s_ready, s * HEADS + n + 1), (probs, s * HEADS + max(n - 3, 0) + CREDIT)]
                        if h % 4 == 0:
                            waits.append((nb_ready, s * 8 + half * 4 + h // 4 + 1))
                        wait_apart(dve, waits)
                        dve.tensor_tensor_reduce(t_sb[:, n % 4, 0:COLS[half]], s_bank[n % 2][:, 0:COLS[half]],
                                                 nb[half][:, h], 1.0, 3e38, ALU.add, ALU.min,
                                                 low[:, n:n + 1]).then_inc(masked, 1)
                    if kind == "T":
                        u = USE["T", n]
                        dve.wait_ge(t_ready, s * USES + u + 1)
                        dve.wait_ge(v_done, s * len(QUADS) + max(n - 1, 0) + CREDIT)
                        dve.tensor_copy(pT[:, n % 2].rearrange("p k q -> p (k q)"), t_bank[u % 2][:])\
                            .then_inc(t_free[u % 2], 1)
                    if kind == "Y":
                        half = n
                        dve.wait_ge(probs, s * HEADS + half * H + H + CREDIT)
                        hs = slice(half * H, half * H + H)
                        chain(dve.reciprocal(recip[:, hs], total[:, hs]))
                        chain.settle()
                        for c in range(2):
                            dve.wait_ge(o_done, s * 4 + half * 2 + c + 1)
                            r = recip[:, half * H + c * 8:half * H + c * 8 + 8].unsqueeze(2).to_broadcast([P, 8, DH])
                            dve.tensor_tensor(o_sb[:, c * 512:c * 512 + 512].rearrange("p (h d) -> p h d", d=DH),
                                              o_bank[c][:].rearrange("p (h d) -> p h d", d=DH), r, ALU.mult)\
                                .then_inc(o_ready, 1)
                    if kind == "W":
                        half = n
                        u = PROJ["out", half]
                        src = p_bank[u % 2][:, 0:D]
                        dve.wait_ge(p_ready, s * PROJS + u + 1)
                        layer_norm_stats(src, half, out_stats)
                        dve.wait_ge(out_rstd, s * 2 + half + 1)
                        dve.tensor_scalar(ln_sb[:, half], src, mv[:, half, 0:1], rstd[:, half:half + 1],
                                          ALU.subtract, ALU.mult).then_inc(p_free[u % 2], 1)
                        dve.wait_ge(p_free[u % 2], s * (PROJS // 2) + u // 2 + 1 + CREDIT)
                        chain(dve.tensor_tensor(ln_sb[:, half], ln_sb[:, half], gain_out[:, layer], ALU.mult))
                        chain.settle()
                        x_t = x_sb[:, bass.ds(tile0 + half, 1), :].rearrange("p a d -> p (a d)")
                        chain(dve.tensor_tensor(x_t, x_t, ln_sb[:, half], ALU.add))
                        chain.settle()
            chain.leave(B)
        moe.vector(dve, chain)

    @block.tensor
    def _(pe):
        pe.wait_ge(loaded["start"], 64)
        pe.wait_ge(loaded["mlp"], 16 * 9)
        for n in range(2):
            pe.matmul(bank[2 + n][:, 0:D], pos_rows[:, n * P:n * P + P], w0b0[:], start=True, stop=True)\
                .then_inc(mlp_pe, 1)
        for layer in range(2):
            pe.wait_ge(mlp_dve, MLP_DVE_SILU[layer])
            for n in range(2):
                pe.transpose(bank[4][:, n * P:n * P + P], mh[:, n], ident[:]).then_inc(mlp_pe, 1)
            pe.wait_ge(mlp_dve, MLP_DVE_T[layer])
            if layer == 0:
                for n in range(2):
                    pe.matmul(bank[2 + n][:, 0:D], mhT[:, n * P:n * P + P], w1[:], start=True, stop=True)\
                        .then_inc(mlp_pe, 1)
            else:
                pe.matmul(bank[5][0:H, 0:N], w2[:], mhT[:], start=True, stop=True).then_inc(mlp_pe, 1)
        for layer in range(2):
            pe.wait_ge(null_ready, 2 + layer)
            if layer == 0:
                pe.wait_ge(mlp_dve, MLP_DVE_TABLE)
            else:
                pe.wait_ge(o_ready, B * 4 + CREDIT)
            for c in range(2):
                ins = pe.transpose(o_bank[0][:, 2 * c:2 * c + 2],
                                   null_split[:, 2 * c:2 * c + 2].rearrange("p a d -> p (a d)").bitcast(F32),
                                   ident[0:2, 0:2])
            ins.then_inc(null_T, 1)
            pe.wait_ge(w_staged, layer + 1)
            pe.wait_ge(null_placed, 2 * (layer + 1))
            with pe.Fori(layer * B, layer * B + B) as s:

                def t_use(n):
                    pe.wait_ge(t_free[n % 2], s * (USES // 2) + n // 2 + CREDIT)
                    return t_bank[n % 2]

                def p_use(n):
                    pe.wait_ge(p_free[n % 2], s * (PROJS // 2) + n // 2 + CREDIT)
                    return p_bank[n % 2]

                for half in range(2):
                    dst = t_use(USE["xn", half])
                    pe.wait_ge(xn_ready, s * 2 + half + 1)
                    pe.transpose(dst[:, 0:P], xn[:, half], ident[:]).then_inc(t_ready, 1)
                for half in range(2):
                    u = USE["xn", half]
                    pe.wait_ge(t_free[u % 2], s * (USES // 2) + u // 2 + 1 + CREDIT)
                    for c, width in ((0, 512), (1, 512), (2, P)):
                        if c < 2:
                            dst = p_use(PROJ["q", half, c])
                        else:
                            pe.wait_ge(masked, (s + 1) * HEADS)
                            dst = s_bank[half]
                        cols = slice(c * 512, c * 512 + width)
                        for n, (lhs, rhs) in enumerate(((xnT_hi, w_hi), (xnT_hi, w_lo), (xnT_lo, w_hi))):
                            ins = pe.matmul(dst[:, 0:width], lhs[:, half], rhs[layer][:, cols],
                                            start=(n == 0), stop=(n == 2))
                        ins.then_inc(p_ready if c < 2 else kv_proj, 1)
                    dst = t_use(USE["k", half])
                    pe.wait_ge(k_split_ready, s * 2 + half + 1)
                    for c in range(2):
                        ins = pe.transpose(dst[:, c * P:c * P + P],
                                           k_split[:, 2 * c:2 * c + 2].rearrange("p a d -> p (a d)").bitcast(F32),
                                           ident[:])
                    ins.then_inc(t_ready, 1)
                    for g in range(4):
                        dst = t_use(USE["q", half, g])
                        if layer == 0:
                            n = PROJ["q", half, g // 2]
                            pe.wait_ge(p_free[n % 2], s * (PROJS // 2) + n // 2 + 1 + CREDIT)
                        else:
                            pe.wait_ge(q_split_ready, (s - B) * 2 + half + 1)
                        for j in range(4):
                            ins = pe.transpose(dst[:, j * P:j * P + P],
                                               q_split[:, 4 * g + j].rearrange("p a d -> p (a d)").bitcast(F32),
                                               ident[:])
                        ins.then_inc(t_ready, 1)
                last = USE["q", 1, 3]
                for slot in range(2):
                    u = last if last % 2 == slot else last - 1
                    pe.wait_ge(t_free[slot], s * (USES // 2) + u // 2 + 1 + CREDIT)
                pe.wait_ge(kv_ready, s * 4 + 4)
                for kind, n in ORDER:
                    if kind == "S":
                        half, h = divmod(n, H)
                        pe.wait_ge(masked, s * HEADS + HEADS + max(n - 1, 0))
                        dst = s_bank[n % 2][:, 0:COLS[half]]
                        pe.matmul(dst, qT[:, half, h], k_hi[:, 0:COLS[half]], start=True, stop=False)
                        pe.matmul(dst, qT[:, half, h], k_lo[:, 0:COLS[half]], start=False, stop=True)\
                            .then_inc(s_ready, 1)
                    if kind == "T":
                        half, first, k = QUADS[n]
                        dst = t_use(USE["T", n])
                        pe.wait_ge(probs, s * HEADS + first + k + CREDIT)
                        for j in range(4):
                            h, kb = (first + j, 0) if half == 0 else (first - H + j // 2, j % 2)
                            ins = pe.transpose(dst[:, j * P:j * P + P], prob[half][:, h, 2 + kb * P:2 + kb * P + P],
                                               ident[:])
                        ins.then_inc(t_ready, 1)
                    if kind == "V":
                        half, first, k = QUADS[n]
                        u = USE["T", n]
                        pe.wait_ge(t_free[u % 2], s * (USES // 2) + u // 2 + 1 + CREDIT)
                        for j in range(4):
                            h, kb = (first + j, 0) if half == 0 else (first - H + j // 2, j % 2)
                            bk = o_bank[h // 8]
                            if h % 8 == 0 and kb == 0:
                                pe.wait_ge(o_ready, s * 4 + half * 2 + CREDIT)
                            ins = pe.matmul(bk[:, (h % 8) * DH:(h % 8) * DH + DH], pT[:, n % 2, j], v_sb[:, kb],
                                            start=(h % 8 == 0 and kb == 0), stop=False, skip_group_check=True)
                        ins.then_inc(v_done, 1)
                    if kind == "Z":
                        dst = t_use(USE["Z", n])
                        pe.wait_ge(probs, s * HEADS + n * H + H + CREDIT)
                        pe.transpose(dst[0:H, 0:P], prob[n][:, :, 0], ident[:]).then_inc(t_ready, 1)
                    if kind == "Y":
                        u = USE["Z", n]
                        pe.wait_ge(t_free[u % 2], s * (USES // 2) + u // 2 + 1 + CREDIT)
                        for c in range(2):
                            pe.matmul(o_bank[c][:], nullT[:], null_v[:, c * 8:c * 8 + 8].rearrange("h a d -> h (a d)"),
                                      start=False, stop=True, skip_group_check=True).then_inc(o_done, 1)
                    if kind == "X":
                        half, c = divmod(n, 2)
                        dst = t_use(USE["X", n])
                        pe.wait_ge(o_ready, s * 4 + half * 2 + c + 1 + CREDIT)
                        for j in range(4):
                            ins = pe.transpose(dst[:, j * P:j * P + P], o_sb[:, (4 * c + j) * P:(4 * c + j) * P + P],
                                               ident[:])
                        ins.then_inc(t_ready, 1)
                    if kind == "W":
                        dst = p_use(PROJ["out", n])
                        for c in range(2):
                            u = USE["X", 2 * n + c]
                            pe.wait_ge(t_free[u % 2], s * (USES // 2) + u // 2 + 1 + CREDIT)
                        for j in range(H // 2):
                            ins = pe.matmul(dst[:, 0:D], oT[:, j], wo[layer][:, j], start=(j == 0),
                                            stop=(j == H // 2 - 1))
                        ins.then_inc(p_ready, 1)
        moe.tensor(pe)


CREDIT = 1
ATTN_LOADS = 12
MLP_DVE_VAR, MLP_DVE_H, MLP_DVE_SILU, MLP_DVE_T, MLP_DVE_TABLE = (2, 7), (3, 8), (4, 9), (5, 10), 11
MLP_PE_H, MLP_PE_T, MLP_PE_TABLE = (2, 6), (4, 8), 9
ACT_CHAIN = (0, 0)
HI = (8, 6)
DVE_CHAIN = (14, 16)


def s_hi(s, layer):
    return B * HI[0] + (s - B) * HI[1]


class Moe:

    WEIGHT_WORDS = 2 * (2 * DOWN_TILES * P + DOWN_TILES * D + 2 * E) + B + B * P + EXPERT_TILES * P + E * E

    def __init__(self, sb, sem, bank, ident, x_sb):
        self.bank, self.ident, self.x_sb = bank, ident, x_sb
        self.w_raw = [sb(f"moe_w{i}", [P, 2, DOWN_TILES, P]) for i in range(2)]
        self.w_down = [sb(f"moe_down{i}", [P, DOWN_TILES, D]) for i in range(2)]
        self.w_token = [sb(f"moe_wt{i}", [D, E]) for i in range(2)]
        self.w_g = [sb(f"moe_wg{i}", [G, E]) for i in range(2)]
        self.gT = sb("moe_gT", [G, B])
        self.g_rep = sb("moe_g_rep", [G, B, P])
        self.sel_raw = sb("moe_sel_raw", [2 * E, EXPERT_TILES, P])
        self.tri = sb("moe_tri", [P, E, E])
        self.loaded = sem("moe_loaded")
        self.attended = sem("attended")
        self.consts = sem("moe_consts")
        self.x_turned, self.x_copied, self.x_hi, self.x_lo = (sem("moe_" + n) for n in
                                                              ("x_turned", "x_copied", "x_hi", "x_lo"))
        self.logits, self.shifted, self.exps = sem("moe_logits"), sem("moe_shifted"), sem("moe_exps")
        self.routed, self.w_turned, self.w_copied = sem("moe_routed"), sem("moe_w_turned"), sem("moe_w_copied")
        self.gate, self.up, self.weight = sem("moe_gate"), sem("moe_up"), sem("moe_weight")
        self.leaked, self.hidden = sem("moe_leaked"), sem("moe_hidden")
        self.y, self.added = sem("moe_y"), sem("moe_added")
        self.out_turned, self.out_ready = sem("moe_out_turned"), sem("moe_out_ready")

    def allocate(self, sb):
        self.w_hi = [sb(f"moe_w_hi{i}", [P, 2, DOWN_TILES, P], F32R) for i in range(2)]
        self.w_lo = [sb(f"moe_w_lo{i}", [P, 2, DOWN_TILES, P], F32R) for i in range(2)]
        self.sel = sb("moe_sel", [2 * E, EXPERT_TILES, P], F32R)
        self.xT = sb("moe_xT", [P, B * N])
        self.xT_hi = sb("moe_xT_hi", [P, B * N], F32R)
        self.xT_lo = sb("moe_xT_lo", [P, B * N], F32R)
        self.score = sb("moe_score", [P, TILES, E])
        self.red = sb("moe_red", [P, TILES])
        self.beats = sb("moe_beats", [P, TILES, E, E])
        self.ties = sb("moe_ties", [P, TILES, E, E])
        self.rank = sb("moe_rank", [P, TILES, E])
        self.w_split = sb("moe_w_split", [P, TILES, 2 * E], F32R)
        self.wT = sb("moe_wT", [2 * E, B * N], F32R)
        self.leak = sb("moe_leak", [P, 2, HALF_T])
        self.hid = sb("moe_hid", [P, DOWN_TILES, HALF_T])

    def load(self, sp, a):
        def dma(dst, src):
            sp.dma_start(dst, src).then_inc(self.loaded, 16)

        for i, name in ((0, "L2_cond_"), (1, "L3_cond_")):
            for n, which in enumerate(("gate", "up")):
                dst = self.w_raw[i][:, n].rearrange("p t m -> p (t m)")
                dma(dst[:, 0:E * M].rearrange("p (e m) -> p e m", e=E),
                    a[name + "w_" + which].rearrange("e h m -> h e m"))
                dma(dst[:, E * M:], a[name + "sw_" + which])
            dma(self.w_down[i][:, 0:EXPERT_TILES],
                a[name + "w_down"].rearrange("e m d -> (e m) d").rearrange("(j p) d -> p j d", p=P))
            dma(self.w_down[i][:, EXPERT_TILES], a[name + "sw_down"])
        for i, name in ((0, "L2_cond_"), (1, "L3_cond_")):
            dma(self.w_token[i][:], a[name + "wtT"])
            dma(self.w_g[i][:], a[name + "wgT"])
        dma(self.gT[:], a["gT"])
        dma(self.sel_raw[:], a["sel"])
        dma(self.tri[:], a["tri"].partition_broadcast(P))

    N_LOADS = 12 + 4 + 3

    def scalar(self, act):
        bank = self.bank
        for layer in range(2):
            if layer == 0:
                for c in range(2):
                    act.wait_ge(self.x_turned, c + 1)
                    act.activation(self.xT_hi[:, c * 512:c * 512 + 512], bank[c][:], ACT.Copy).then_inc(self.x_hi, 1)
            else:
                act.wait_ge(self.added, 2 + CREDIT)
                act.activation(self.xT_hi[:], self.xT[:], ACT.Copy).then_inc(self.x_hi, 2)
            act.wait_ge(self.shifted, layer + 1)
            act.activation(self.score[:], self.score[:], ACT.Exp).then_inc(self.exps, 1)
            with act.Fori(2 * layer, 2 * layer + 2) as v:
                for m in range(DOWN_TILES):
                    act.wait_ge(self.gate, v * DOWN_TILES + m + 1)
                    act.activation(self.leak[:, m % 2], bank[4 + m % 2][:], ACT.Copy, scale=0.01)\
                        .then_inc(self.leaked, 1)
        for c in range(2):
            act.wait_ge(self.out_turned, c + 1)
            act.activation(self.leak[:, c], bank[c][:], ACT.Copy).then_inc(self.out_ready, 1)

    def prepare(self, dve, chain):
        dve.wait_ge(self.loaded, 16 * self.N_LOADS)
        dve.tensor_copy(self.g_rep[:], self.gT[:].unsqueeze(2).to_broadcast([G, B, P])).then_inc(self.consts, 1)
        dve.tensor_copy(self.sel[:], self.sel_raw[:]).then_inc(self.consts, 1)
        for i in range(2):
            chain(dve.tensor_copy(self.w_hi[i][:], self.w_raw[i][:]))
            chain.settle()
            dve.tensor_tensor(self.w_lo[i][:], self.w_raw[i][:], self.w_hi[i][:].bitcast(F32), ALU.subtract)\
                .then_inc(self.consts, 1)

    def vector(self, dve, chain):
        bank, score, red = self.bank, self.score, self.red

        def over(x):
            return x.unsqueeze(2).to_broadcast([P, TILES, E])

        chain.settle()
        dve.sem_inc(self.attended, 1)
        self.prepare(dve, chain)
        for layer in range(2):
            if layer == 0:
                for c in range(2):
                    cols = slice(c * 512, c * 512 + 512)
                    dve.wait_ge(self.x_hi, c + 1)
                    dve.tensor_copy(self.xT[:, cols], bank[c][:]).then_inc(self.x_copied, 1)
            dve.wait_ge(self.x_hi, 2 * layer + 2)
            if layer == 0:
                dve.wait_ge(self.x_copied, 2)
            dve.tensor_tensor(self.xT_lo[:], self.xT[:], self.xT_hi[:].bitcast(F32), ALU.subtract)\
                .then_inc(self.x_lo, 1)
            dve.wait_ge(self.logits, layer + 1)
            lg = bank[2][:, 0:TILES * E].rearrange("p (t e) -> p t e", e=E)
            chain(dve.tensor_scalar(score[:], lg, 0.5, None, ALU.mult))
            chain.settle()
            chain(dve.tensor_reduce(red[:], score[:], AX.X, ALU.max))
            chain.settle()
            dve.tensor_tensor(score[:], score[:], over(red[:]), ALU.subtract).then_inc(self.shifted, 1)
            dve.wait_ge(self.exps, layer + 1)
            chain(dve.tensor_reduce(red[:], score[:], AX.X, ALU.add))
            chain.settle()
            chain(dve.reciprocal(red[:], red[:]))
            chain.settle()
            chain(dve.tensor_tensor(score[:], score[:], over(red[:]), ALU.mult))
            chain.settle()
            mine = score[:].unsqueeze(3).to_broadcast([P, TILES, E, E])
            others = score[:].unsqueeze(2).to_broadcast([P, TILES, E, E])
            chain(dve.tensor_tensor(self.beats[:], others, mine, ALU.is_gt))
            chain(dve.tensor_tensor(self.ties[:], others, mine, ALU.is_equal))
            chain.settle()
            chain(dve.tensor_tensor(self.ties[:], self.ties[:],
                                    self.tri[:].unsqueeze(1).to_broadcast([P, TILES, E, E]), ALU.mult))
            chain.settle()
            chain(dve.tensor_tensor(self.beats[:], self.beats[:], self.ties[:], ALU.add))
            chain.settle()
            chain(dve.tensor_reduce(self.rank[:], self.beats[:], AX.X, ALU.add))
            chain.settle()
            chain(dve.tensor_scalar(self.rank[:], self.rank[:], 2.0, None, ALU.is_lt))
            chain.settle()
            chain(dve.tensor_tensor(score[:], score[:], self.rank[:], ALU.mult))
            chain.settle()
            chain(dve.tensor_reduce(red[:], score[:], AX.X, ALU.add))
            chain.settle()
            chain(dve.tensor_scalar(red[:], red[:], 1e-20, None, ALU.add))
            chain.settle()
            chain(dve.reciprocal(red[:], red[:]))
            chain.settle()
            chain(dve.tensor_tensor(score[:], score[:], over(red[:]), ALU.mult))
            chain.settle()
            chain(dve.tensor_copy(self.w_split[:, :, 0:E], score[:]))
            chain.settle()
            dve.tensor_tensor(self.w_split[:, :, E:], score[:], self.w_split[:, :, 0:E].bitcast(F32), ALU.subtract)\
                .then_inc(self.routed, 1)
            for c in range(2):
                dve.wait_ge(self.w_turned, 2 * layer + c + 1)
                dve.tensor_copy(self.wT[:, c * 512:c * 512 + 512], bank[2 + c][0:2 * E, :])\
                    .then_inc(self.w_copied, 1)
            with dve.Fori(2 * layer, 2 * layer + 2) as v:
                chain.enter(v - 2 * layer, 2 * DOWN_TILES - 1)
                for m in range(DOWN_TILES):
                    hid = self.hid[:, m]
                    dve.wait_ge(self.leaked, v * DOWN_TILES + m + 1)
                    chain(dve.tensor_tensor(hid, bank[4 + m % 2][:], self.leak[:, m % 2], ALU.max))
                    chain.settle()
                    dve.wait_ge(self.up, v * DOWN_TILES + m + 1)
                    ins = dve.tensor_tensor(hid, hid, bank[6 + m % 2][:], ALU.mult)
                    if m < EXPERT_TILES:
                        chain(ins)
                        chain.settle()
                        dve.wait_ge(self.weight, v * EXPERT_TILES + m + 1)
                        ins = dve.tensor_tensor(hid, hid, bank[2 + m % 2][:], ALU.mult)
                    ins.then_inc(self.hidden, 1)
                dve.wait_ge(self.y, v + 1)
                x = self.xT[:, bass.ds((v - 2 * layer) * HALF_T, HALF_T)]
                dve.tensor_tensor(x, x, bank[0][:], ALU.add).then_inc(self.added, 1)
            chain.leave(2)

    def gpsimd(self, pool):
        pass

    def tensor(self, pe):
        bank, ident = self.bank, self.ident
        pe.wait_ge(self.attended, 1)
        for layer in range(2):
            if layer == 0:
                for t in range(TILES):
                    ins = pe.transpose(bank[t // 4][:, (t % 4) * P:(t % 4) * P + P], self.x_sb[:, t], ident[:])
                    if t % 4 == 3:
                        ins.then_inc(self.x_turned, 1)
                pe.wait_ge(self.x_copied, 2)
                pe.wait_ge(self.consts, 4)
            else:
                pe.wait_ge(self.added, 2 + CREDIT)
            for t in range(TILES):
                dst = bank[2][:, t * E:t * E + E]
                pe.matmul(dst, self.xT[:, t * P:t * P + P], self.w_token[layer][:], start=True, stop=False)
                ins = pe.matmul(dst, self.g_rep[:, t // 2], self.w_g[layer][:], start=False, stop=True)
            ins.then_inc(self.logits, 1)
            pe.wait_ge(self.routed, layer + 1)
            for t in range(TILES):
                ins = pe.transpose(bank[2 + t // 4][0:2 * E, (t % 4) * P:(t % 4) * P + P],
                                   self.w_split[:, t].bitcast(F32), ident[:])
                if t % 4 == 3:
                    ins.then_inc(self.w_turned, 1)
            pe.wait_ge(self.w_copied, 2 * layer + 2)
            pe.wait_ge(self.x_lo, layer + 1)
            with pe.Fori(2 * layer, 2 * layer + 2) as v:
                cols = bass.ds((v - 2 * layer) * HALF_T, HALF_T)

                def down(m):
                    pe.wait_ge(self.hidden, v * DOWN_TILES + m + 1 + CREDIT)
                    if m == 0:
                        pe.wait_ge(self.added, v + CREDIT)
                    return pe.matmul(bank[0][:], self.w_down[layer][:, m], self.hid[:, m], start=(m == 0),
                                     stop=(m == DOWN_TILES - 1))

                for m in range(DOWN_TILES):
                    pe.wait_ge(self.hidden, v * DOWN_TILES + max(m - 1, 0) + CREDIT)
                    for n, (base, ready) in enumerate(((4, self.gate), (6, self.up))):
                        w_hi, w_lo = self.w_hi[layer][:, n, m], self.w_lo[layer][:, n, m]
                        dst = bank[base + m % 2][:]
                        pe.matmul(dst, w_hi, self.xT_hi[:, cols], start=True, stop=False)
                        pe.matmul(dst, w_hi, self.xT_lo[:, cols], start=False, stop=False)
                        pe.matmul(dst, w_lo, self.xT_hi[:, cols], start=False, stop=True).then_inc(ready, 1)
                    if m < EXPERT_TILES:
                        pe.matmul(bank[2 + m % 2][:], self.sel[:, m], self.wT[:, cols], start=True, stop=True)\
                            .then_inc(self.weight, 1)
                    if m >= 1:
                        down(m - 1)
                down(DOWN_TILES - 1).then_inc(self.y, 1)
        pe.wait_ge(self.added, 4 + CREDIT)
        for t in range(TILES):
            ins = pe.transpose(bank[t // 4][:, (t % 4) * P:(t % 4) * P + P], self.xT[:, t * P:t * P + P], ident[:])
            if t % 4 == 3:
                ins.then_inc(self.out_turned, 1)

    def store(self, sp, out, stored):
        for c in range(2):
            sp.wait_ge(self.out_ready, c + 1)
            sp.dma_start(out.rearrange("(c t p) d -> c p t d", p=P, t=4)[c],
                         self.leak[:, c].rearrange("p (t d) -> p t d", d=D)).then_inc(stored, 16)
        sp.wait_ge(stored, 32)


def moe_arrays(g):
    arrays = {"gT": g["cond_64"].T}
    sel = np.zeros((2, E, EXPERT_TILES, 2, M), np.float32)
    for e in range(E):
        sel[:, e, e // 2, e % 2] = 1
    arrays["sel"] = sel.reshape(2 * E, EXPERT_TILES, P)
    arrays["tri"] = np.tril(np.ones((E, E), np.float32), -1)
    for name in ("L2_cond_", "L3_cond_"):
        for w in ("w_gate", "w_up", "w_down", "sw_gate", "sw_up", "sw_down"):
            arrays[name + w] = g[name + w]
        arrays[name + "wtT"] = g[name + "wt"].T
        arrays[name + "wgT"] = g[name + "wg"].T
    return arrays


def kernel(**inputs):
    import concourse.bacc as bacc
    from concourse.bass_utils import run_bass_kernel_spmd

    g = {n: np.asarray(v) for n, v in inputs.items()}
    cond = g["cond_64"]
    null_key_rows = np.zeros((2, DH), np.float32)
    null_key_rows[0] = cond[0]
    null_v_blocks = np.zeros((H, H, DH), np.float32)
    for h in range(H):
        null_v_blocks[h, h] = cond[1]
    pos_rows = np.ones((2, N), np.float32)
    pos_rows[0] = np.arange(N - 1, -1, -1)
    arrays = {
        "x": g["x"].reshape(B * N, D),
        "bias": g["fside_16xSxS_0"],
        "mask0": g["mask_BxS_bk0"],
        "mask1": g["mask_BxS_bf1"],
        "ident": np.eye(P, dtype=np.float32),
        "null_key_rows": null_key_rows,
        "null_v_blocks": null_v_blocks.reshape(H, INNER),
        "pos_rows": pos_rows,
    }
    for name in ("L0_cond_g_in", "L0_cond_null_attn_bias", "L0_cond_Wq", "L0_cond_Wkv", "L0_cond_Wo",
                 "L0_cond_g_out", "L1_cond_g_norm", "L1_cond_Wq", "L1_cond_Wkv", "L1_cond_q_scale",
                 "L1_cond_k_scale", "L1_cond_null_attn_bias", "L1_cond_w0", "L1_cond_b0", "L1_cond_g0",
                 "L1_cond_w1", "L1_cond_b1", "L1_cond_g1", "L1_cond_w2", "L1_cond_b2", "L1_cond_Wout",
                 "L1_cond_g_out"):
        arrays[name] = g[name]
    arrays.update(moe_arrays(g))
    arrays = {n: np.ascontiguousarray(v) for n, v in arrays.items()}

    nc = bacc.Bacc("TRN2", target_bir_lowering=False, num_devices=1)
    aps = {n: nc.dram_tensor("in_" + n, v.shape, mybir.dt.from_np(v.dtype), kind="ExternalInput").ap()
           for n, v in arrays.items()}
    out = nc.dram_tensor("out", (B * N, D), F32, kind="ExternalOutput").ap()
    build(nc, aps, out)
    r = run_bass_kernel_spmd(nc, [{"in_" + n: v for n, v in arrays.items()}], core_ids=[0])
    return r.results[0]["out"].reshape(B, N, D)
```

```python
from contextlib import ExitStack

import numpy as np

import concourse.bass as bass
from concourse import mybir

F32 = mybir.dt.float32
F32R = mybir.dt.float32r
U8 = mybir.dt.uint8
ALU = mybir.AluOpType
ACT = mybir.ActivationFunctionType
AX = mybir.AxisListType

P = 128
B, N, D = 4, 256, 128
H, DH = 16, 64
INNER = H * DH
TILES = B * N // P
COLS = (P + 2, 2 * P + 2)
E, M, SM, G = 8, 64, 128, 64
EPS = 1e-5
FAR = 1e30
CUT = 2
HEADS = 2 * H
HALF_T = 512
EXPERT_TILES = E * M // P
DOWN_TILES = EXPERT_TILES + 1


STEP = {"T": 3, "Z": 4, "V": 5, "Y": 6, "X": 8, "X2": 10, "W": 12, "out": 13,
        "stats": 0, "norm": 1, "xn": 2, "kv": 5, "q0": 5, "q1": 6, "sums": 6, "apply": 10, "split": 10,
        "g0": 10, "g1": 11, "g2": 12, "g3": 13, "K0": 2, "K1": 5, "k0": 2}


def attention_order():
    at = {}

    def put(step, kind, n):
        at.setdefault(step % HEADS, []).append((kind, n, step >= HEADS))

    quads = [(0, 4 * g, 4) for g in range(4)] + [(1, H + 2 * g, 2) for g in range(8)]
    for i in range(HEADS):
        put(i, "S", i)
    for n, (half, first, k) in enumerate(quads):
        put(first + k - 1 + STEP["T"], "T", n)
    for half in range(2):
        put(half * H + H - 1 + STEP["Z"], "Z", half)
    for n, (half, first, k) in enumerate(quads):
        put(first + k - 1 + STEP["V"], "V", n)
    put(4, "v", 0)
    for half in range(2):
        last = half * H + H - 1
        put(last + STEP["Y"], "Y", half)
        put(last + STEP["X"], "X", 2 * half)
        put(last + STEP["X2"], "X", 2 * half + 1)
        put(last + STEP["W"], "W", half)
        put(last + STEP["out"], "out", half)
        n, first = 1 - half, half * H
        for kind in ("stats", "norm", "xn", "kv", "q0", "q1", "sums", "apply", "split"):
            put(first + STEP[kind], kind, n)
        for g in range(4):
            put(first + STEP[f"g{g}"], "q", 4 * n + g)
    put(5, "v", 1)
    put(H - STEP["K1"], "K", 1)
    put(HEADS - STEP["K0"], "K", 0)
    put(STEP["k0"], "k0", 0)
    return quads, [item for i in range(HEADS) for item in at[i]]


QUADS, ORDER = attention_order()
TURNED_BY_ACT = (1, 4, 6, 7, 8, 10, 11)
PREPARES = ("stats", "norm", "xn", "kv", "q0", "q1", "sums", "apply", "split", "q", "K")


def prepares_next(item):
    kind, n, late = item
    return kind in PREPARES and (n < 4 if kind == "q" else n == 0) and not late


LAST = 2 * B
FIRST_ONLY = {2: ("h", 0), 4: ("hn", 0), 6: ("hs", 0), 7: ("ht", 0), 9: ("h", 1), 11: ("hn", 1), 13: ("hs", 1),
              14: ("ht", 1), 16: ("table", 0), 20: ("w1", 0)}


def turn(s):
    if not isinstance(s, int):
        return ORDER
    order = []
    for it in ORDER:
        order.append(it)
        if s == 0 and it[0] == "S" and it[1] in FIRST_ONLY:
            order.append((*FIRST_ONLY[it[1]], False))
    return [it for it in order if (prepares_next(it) or s >= 0) and (not it[2] or s > 0) and (it[2] or s < LAST)
            and (not prepares_next(it) or s < LAST - 1)]


class Ring:

    def __init__(self, kinds):
        self.kinds = kinds
        self.steady = len(self.items(1))
        assert self.steady % 2 == 0

    def items(self, s):
        return [it for it in turn(s) if it[0] in self.kinds]

    def use(self, s, kind, n, late=False):
        if isinstance(s, int) and (s < 1 or s > LAST - 2):
            before = sum(len(self.items(i)) for i in range(-1, s))
            count = before + self.items(s).index((kind, n, late))
            return count, count // 2, count % 2
        c = sum(len(self.items(i)) for i in (-1, 0)) - self.steady + self.items(1).index((kind, n, late))
        return s * self.steady + c, s * (self.steady // 2) + c // 2, c % 2


T_RING = Ring(("xn", "q", "K", "T", "Z", "X", "h", "ht", "table"))
P_RING = Ring(("kv", "q0", "q1", "W"))


def late(kind, n):
    return (kind, n, True) in ORDER


class Chain:

    def __init__(self, eng, sem):
        self.eng, self.sem, self.base, self.n = eng, sem, 0, 0

    def __call__(self, instruction):
        instruction.then_inc(self.sem, 1)
        self.n += 1
        return instruction

    def settle(self):
        self.eng.wait_ge(self.sem, self.base + self.n)

    def enter(self, iteration, per_iteration):
        self.before, self.per = self.base + self.n, per_iteration
        self.base, self.n = self.before + iteration * per_iteration, 0

    def leave(self, iterations):
        assert self.n == self.per, (self.n, self.per)
        self.base, self.n = self.before + iterations * self.per, 0


def build(nc, a, out):
    with ExitStack() as ctx:
        _build(nc, ctx, a, out)


def _build(nc, ctx, a, out):
    def sb(name, shape, dt=F32):
        return ctx.enter_context(nc.sbuf_tensor("sb_" + name, shape, dt))

    def sem(name):
        return ctx.enter_context(nc.semaphore(name))

    bank = [ctx.enter_context(nc.psum_tensor(f"bank{i}", [P, 512], F32)) for i in range(8)]
    s_bank, t_bank, o_bank, p_bank = bank[0:2], bank[2:4], bank[4:6], bank[6:8]

    ident = sb("ident", [P, P])
    x_sb = sb("x", [P, TILES, D])
    with ExitStack() as first:
        bias0 = first.enter_context(nc.sbuf_tensor("sb_bias0", [P, H, P], F32))
        bias1 = first.enter_context(nc.sbuf_tensor("sb_bias1", [P, H, N], F32))
    moe = Moe(sb, sem, bank, ident, x_sb)
    sb("rest_of_bias", [P, H * (P + N) - Moe.WEIGHT_WORDS])
    attention = ctx.enter_context(ExitStack())
    permanent = sb

    def sb(name, shape, dt=F32):
        return attention.enter_context(nc.sbuf_tensor("sb_" + name, shape, dt))

    wqkv = sb("wqkv", [P, INNER + P])
    w_hi = [sb(f"w_hi{i}", [P, INNER + P], F32R) for i in range(2)]
    w_lo = [sb(f"w_lo{i}", [P, INNER + P], F32R) for i in range(2)]
    wo = [sb(f"wo{i}", [P, H // 2, D]) for i in range(2)]
    gain_in = sb("gain_in", [P, 2])
    gain_out = sb("gain_out", [P, 2, D])
    qk_scale = sb("qk_scale", [P, 2, DH])
    k_gain = sb("k_gain", [P, DH])
    null_kv = sb("null_kv", [2, DH])
    null_k = sb("null_k", [2, 2, DH])
    null_split = sb("null_split", [2, 2, 4, DH], F32R)
    null_cols = sb("null_cols", [P, 2, 2, 2], F32R)
    null_s = sb("null_s", [2, 4])
    null_v = sb("null_v", [H, H, DH])
    null_bias = sb("null_bias", [P, 2, H])
    mask_u8 = sb("mask_u8", [P, 2, B, N], U8)
    mask = sb("mask", [P, 2, B, N])
    toep = sb("toep", [P, H, N])
    nb = [sb("nb0", [P, H, COLS[0]]), sb("nb1", [P, H, COLS[1]])]
    minus_half = sb("minus_half", [P, 2 * H + 2])
    stats = sb("stats", [P, 6])
    mv = sb("mv", [P, 2, 2])
    var_e = sb("var_e", [P, 2])
    rstd = sb("rstd", [P, 2])
    out_st = sb("out_st", [P, 6])
    out_mv = sb("out_mv", [P, 2, 2])
    out_var = sb("out_var", [P, 2])
    out_r = sb("out_r", [P, 2])
    xn = sb("xn", [P, 2, D])
    xnT_hi = sb("xnT_hi", [P, 2, P], F32R)
    xnT_lo = sb("xnT_lo", [P, 2, P], F32R)
    sq = sb("sq", [P, INNER + DH])
    ss = sb("ss", [P, 2, H + 1])
    rq = sb("rq", [P, 2, H + 1])
    qn = sb("qn", [P, H, DH])
    q_split = sb("q_split", [P, H, 2, DH], F32R)
    kv = sb("kv", [P, 2, P])
    kn = sb("kn", [P, DH])
    k_split = sb("k_split", [P, 4, DH], F32R)
    qT = sb("qT", [P, 2, H, P], F32R)
    k0_hi = sb("k0_hi", [P, COLS[0]], F32R)
    k0_lo = sb("k0_lo", [P, COLS[0]], F32R)
    k_hi = sb("k_hi", [P, COLS[1]], F32R)
    k_lo = sb("k_lo", [P, COLS[1]], F32R)
    v_sb = sb("v", [P, 2, DH])
    t_sb = sb("t", [P, 4, COLS[1]])
    low = sb("low", [P, HEADS])
    total = sb("total", [P, HEADS])
    recip = sb("recip", [P, HEADS])
    prob = [sb("prob0", [P, H, COLS[0]]), sb("prob1", [P, H, COLS[1]])]
    pT = sb("pT", [P, 2, 4, P])
    nullT = sb("nullT", [H, P])
    o_sb = sb("o", [P, INNER])
    oT = sb("oT", [P, H // 2, P])
    ln_sb = sb("ln", [P, 2, D])
    pos_rows = sb("pos_rows", [2, N])
    w0b0 = sb("w0b0", [2, D])
    mlp_rows = sb("mlp_rows", [P, 3, D])
    w1 = sb("w1", [D, D])
    w2 = sb("w2", [D, H])
    b2 = sb("b2", [H, 1])
    mlp_mv = sb("mlp_mv", [P, 2, 2])
    mlp_var = sb("mlp_var", [P, 2])
    mlp_r = sb("mlp_r", [P, 2])
    flat = qn[:].rearrange("p h d -> p (h d)")
    me = flat[:, 0:2 * D].rearrange("p (n d) -> p n d", d=D)
    mhT = flat[:, 2 * D:2 * D + N]
    mh = flat[:, 2 * D + N:4 * D + N].rearrange("p (n d) -> p n d", d=D)
    table = sb("table", [H, N + P])
    scratch = nc.dram_tensor("bias_table", [H, P, N + P], F32, kind="Internal").ap()

    loaded = {n: sem("loaded_" + n) for n in ("x", "start", "wo", "mlp", "wqkv0", "wqkv1", "attn", "bias0", "bias1", "moe")}
    dve_step, act_step, pool_step = sem("dve_step"), sem("act_step"), sem("pool_step")
    w_staged = sem("w_staged")
    consts_ready = sem("consts_ready")
    mlp_dve, mlp_act, mlp_pool = sem("mlp_dve"), sem("mlp_act"), sem("mlp_pool")
    table_stored, toep_loaded, bias_cut = sem("table_stored"), sem("toep_loaded"), sem("bias_cut")
    null_ready, null_T, null_placed = sem("null_ready"), sem("null_T"), sem("null_placed")
    null_scaled = sem("null_scaled")
    stats_ready, rstd_ready = sem("stats_ready"), sem("rstd_ready")
    xn_ready, xnT_ready = sem("xn_ready"), sem("xnT_ready")
    t_ready = sem("t_ready")
    t_free = [sem("t_free0"), sem("t_free1")]
    p_ready = sem("p_ready")
    p_free = [sem("p_free0"), sem("p_free1")]
    xn_hi, q_hi, k_hi_done = sem("xn_hi"), sem("q_hi"), sem("k_hi_done")
    sq_done, norms_ready, rq_ready = sem("sq_done"), sem("norms_ready"), sem("rq_ready")
    qn_ready, q_split_ready, k_split_ready = sem("qn_ready"), sem("q_split_ready"), sem("k_split_ready")
    kv_copied, k_placed, v_placed = sem("kv_copied"), sem("k_placed"), sem("v_placed")
    k0_copied = sem("k0_copied")
    s_ready, masked, probs = sem("s_ready"), sem("masked"), sem("probs")
    nb_ready = sem("nb_ready")
    pT_ready, v_done = sem("pT_ready"), sem("v_done")
    nullT_ready, o_done, o_ready, oT_ready = sem("nullT_ready"), sem("o_done"), sem("o_ready"), sem("oT_ready")
    out_stats, out_rstd, tile_done = sem("out_stats"), sem("out_rstd"), sem("tile_done")
    stored = sem("stored")
    passed = sem("passed")

    attention.close()
    moe.allocate(permanent)

    def wait_apart(eng, waits):
        for which, value in waits:
            eng.wait_ge(which, value)
        eng.sem_inc(passed, 1)

    block = ctx.enter_context(nc.Block())

    CONSTS = 5

    @block.sync
    def _(sp):
        for given_back in (*t_free, *p_free, v_done, probs, o_ready, moe.hidden, moe.added):
            sp.sem_inc(given_back, CREDIT)
        sp.dma_start(x_sb[:], a["x"].rearrange("(t p) d -> p t d", p=P)).then_inc(loaded["x"], 16)
        sp.dma_start(wqkv[:, 0:INNER], a["L0_cond_Wq"]).then_inc(loaded["wqkv0"], 16)
        sp.dma_start(wqkv[:, INNER:], a["L0_cond_Wkv"]).then_inc(loaded["wqkv0"], 16)
        sp.dma_start(bias0[:], a["bias"][:, 0:P, 0:P].rearrange("h q k -> q h k")).then_inc(loaded["bias0"], 16)
        sp.dma_start(bias1[:], a["bias"][:, P:N, :].rearrange("h q k -> q h k")).then_inc(loaded["bias1"], 16)
        sp.wait_ge(w_staged, 1)
        sp.dma_start(wqkv[:, 0:INNER], a["L1_cond_Wq"]).then_inc(loaded["wqkv1"], 16)
        sp.dma_start(wqkv[:, INNER:], a["L1_cond_Wkv"]).then_inc(loaded["wqkv1"], 16)
        _, pairs, slot = T_RING.use(0, "table", 0)
        sp.wait_ge(t_free[slot], pairs + 1 + CREDIT)
        sp.dma_start(scratch, table[:].unsqueeze(1).to_broadcast([H, P, N + P])).then_inc(table_stored, 16)
        sp.wait_ge(table_stored, 16)
        sp.dma_start(toep[:], bass.AP(tensor=scratch.tensor, offset=P - 1,
                                      ap=[[N + P - 1, P], [P * (N + P), H], [1, N]])).then_inc(toep_loaded, 16)
        sp.wait_ge(nb_ready, B * HEADS // CUT)
        moe.load(sp, a)
        moe.store(sp, out, stored)

    @block.scalar
    def _(act):
        act.dma_start(gain_in[:, 0:1], a["L0_cond_g_in"].rearrange("(d o) -> d o", o=1)).then_inc(loaded["start"], 16)
        act.dma_start(ident[:], a["ident"]).then_inc(loaded["start"], 16)
        act.dma_start(mask_u8[:, 0], a["mask0"].partition_broadcast(P)).then_inc(loaded["start"], 16)
        act.dma_start(mask_u8[:, 1], a["mask1"].partition_broadcast(P)).then_inc(loaded["start"], 16)
        loads = [
            (gain_in[:, 1:2], a["L1_cond_g_norm"].rearrange("(d o) -> d o", o=1)),
            (gain_out[:, 0], a["L0_cond_g_out"].partition_broadcast(P)),
            (gain_out[:, 1], a["L1_cond_g_out"].partition_broadcast(P)),
            (qk_scale[:, 0], a["L1_cond_q_scale"].partition_broadcast(P)),
            (qk_scale[:, 1], a["L1_cond_k_scale"].partition_broadcast(P)),
            (null_bias[:, 0], a["L0_cond_null_attn_bias"].partition_broadcast(P)),
            (null_bias[:, 1], a["L1_cond_null_attn_bias"].partition_broadcast(P)),
            (null_kv[:], a["null_key_rows"]),
            (null_v[:].rearrange("h a d -> h (a d)"), a["null_v_blocks"]),
        ]
        assert len(loads) == ATTN_LOADS
        for dst, src in loads:
            act.dma_start(dst, src).then_inc(loaded["attn"], 16)
        act.dma_start(pos_rows[:], a["pos_rows"]).then_inc(loaded["mlp"], 16)
        act.dma_start(w0b0[0:1, :], a["L1_cond_w0"]).then_inc(loaded["mlp"], 16)
        act.dma_start(w0b0[1:2, :], a["L1_cond_b0"].rearrange("(o d) -> o d", o=1)).then_inc(loaded["mlp"], 16)
        for n, name in enumerate(("g0", "g1", "b1")):
            act.dma_start(mlp_rows[:, n], a["L1_cond_" + name].partition_broadcast(P)).then_inc(loaded["mlp"], 16)
        act.dma_start(w1[:], a["L1_cond_w1"]).then_inc(loaded["mlp"], 16)
        act.dma_start(w2[:], a["L1_cond_w2"]).then_inc(loaded["mlp"], 16)
        act.dma_start(b2[:], a["L1_cond_b2"].rearrange("(h o) -> h o", o=1)).then_inc(loaded["mlp"], 16)
        act.dma_start(wo[0][:], a["L0_cond_Wo"].rearrange("(j p) d -> p j d", p=P)).then_inc(loaded["wo"], 16)
        act.dma_start(wo[1][:], a["L1_cond_Wout"].rearrange("(j p) d -> p j d", p=P)).then_inc(loaded["wo"], 16)
        def q_high(s, n, c):
            _, pairs, slot = P_RING.use(s, f"q{c}", n)
            act.wait_ge(p_free[slot], pairs + 1 + CREDIT)
            hs = slice(c * 8, c * 8 + 8)
            act.activation(q_split[:, hs, 0], qn[:, hs], ACT.Copy).then_inc(q_hi, 1)

        def answer(s, layer, tail_layer, next_layer):
            for kind, n, is_late in turn(s):
                b = s - 1 if is_late else s
                tile = 2 * s + 2 - n
                if kind in ("xn", "q", "K", "T", "Z", "X"):
                    count, pairs, slot = T_RING.use(s, kind, n, is_late)
                    src = t_bank[slot]
                if kind in ("kv", "q0", "q1"):
                    count, pairs, slot = P_RING.use(s, kind, n, is_late)
                    src = p_bank[slot]
                    lay = layer if n == 1 else next_layer
                before = (s - 1, 0) if n == 1 else (s, 1)
                first = isinstance(s, int) and s < 0
                if kind == "xn":
                    act.wait_ge(t_ready, count + 1)
                    act.activation(xnT_hi[:, n], src[:, 0:P], ACT.Copy).then_inc(xn_hi, 1)
                if kind == "kv":
                    act.wait_ge(p_ready, count + 1)
                    if not first and not (isinstance(s, int) and s == 0 and n == 1):
                        act.wait_ge(v_placed, tile - 1)
                        act.wait_ge(qn_ready, tile - 1)
                    act.activation(kv[:, n], src[:, 0:P], ACT.Copy).then_inc(kv_copied, 1)
                    act.wait_ge(kv_copied, tile + 1)
                    act.sem_inc(p_free[slot], 1)
                    if lay == 1:
                        if not (isinstance(s, int) and s == B - 1):
                            act.wait_ge(norms_ready, tile - 2 * B)
                        act.activation(sq[:, INNER:], kv[:, n, 0:DH], ACT.Square).then_inc(sq_done, 1)
                if kind in ("q0", "q1"):
                    c = int(kind[1])
                    act.wait_ge(p_ready, count + 1)
                    if lay == 0:
                        if not first:
                            act.wait_ge(t_ready, T_RING.use(before[0], "q", 4 * before[1] + 3)[0] + 1)
                        act.activation(q_split[:, c * 8:c * 8 + 8, 0], src[:].rearrange("p (h d) -> p h d", d=DH),
                                       ACT.Copy).then_inc(q_hi, 1)
                    else:
                        act.activation(sq[:, c * 512:c * 512 + 512], src[:], ACT.Square).then_inc(sq_done, 1)
                if kind == "hn":
                    act.wait_ge(mlp_dve, MLP_DVE_H[n])
                    act.activation(me, mh, ACT.Exp, scale=-1.0).then_inc(mlp_act, 1)
                if kind == "split":
                    lay = layer if n == 1 else next_layer
                    if lay == 1:
                        act.wait_ge(t_ready, T_RING.use(before[0], "q", 4 * before[1] + 3)[0] + 1)
                        q_high(s, n, 0)
                    act.wait_ge(qn_ready, tile + 1)
                    if not first:
                        act.wait_ge(t_ready, T_RING.use(before[0], "K", before[1])[0] + 1)
                    act.activation(k_split[:, 0:2], kn[:].unsqueeze(1).to_broadcast([P, 2, DH]), ACT.Copy)\
                        .then_inc(k_hi_done, 1)
                    if lay == 1:
                        q_high(s, n, 1)
                if kind == "q" and n % 2 == 0:
                    act.wait_ge(t_ready, count + 1)
                    act.activation(qT[:, n // 4, 4 * (n % 4):4 * (n % 4) + 4].rearrange("p h q -> p (h q)"), src[:],
                                   ACT.Copy).then_inc(t_free[slot], 1)
                if kind == "K":
                    act.wait_ge(t_ready, count + 1)
                    to_hi, to_lo = (k0_hi[:, 2:], k0_lo[:, 2:]) if n == 0 else (k_hi[:, 2 + P:], k_lo[:, 2 + P:])
                    act.activation(to_hi, src[:, 0:P], ACT.Copy).then_inc(k_placed, 1)
                    act.activation(to_lo, src[:, P:2 * P], ACT.Copy).then_inc(t_free[slot], 1)
                if kind == "k0":
                    if not (isinstance(s, int) and s == 0):
                        act.wait_ge(s_ready, s * HEADS)
                    act.wait_ge(k_placed, 2 * s + 1)
                    _, pairs, slot = T_RING.use(s - 1, "K", 0)
                    act.wait_ge(t_free[slot], pairs + 1 + CREDIT)
                    act.activation(k_hi[:, 2:2 + P], k0_hi[:, 2:], ACT.Copy).then_inc(k0_copied, 1)
                    act.activation(k_lo[:, 2:2 + P], k0_lo[:, 2:], ACT.Copy).then_inc(k0_copied, 1)
                if kind == "v":
                    tile = 2 * s + n
                    if not (isinstance(s, int) and s == 0):
                        act.wait_ge(v_done, s * len(QUADS) + CREDIT)
                    act.wait_ge(kv_copied, tile + 1)
                    act.activation(v_sb[:, n], kv[:, n, DH:P], ACT.Copy).then_inc(v_placed, 1)
                if kind == "S":
                    half, h = divmod(n, H)
                    act.wait_ge(masked, s * HEADS + HEADS + n + 1)
                    act.activation(prob[half][:, h], t_sb[:, n % 4, 0:COLS[half]], ACT.Exp, scale=-1.0,
                                   bias=low[:, n:n + 1], accum_out=total[:, n:n + 1]).then_inc(probs, 1)
                if kind == "T" and n in TURNED_BY_ACT:
                    act.wait_ge(t_ready, count + 1)
                    if not (first_turn(s) and n < 2):
                        act.wait_ge(v_done, b * len(QUADS) + n - 1 + CREDIT)
                    act.activation(pT[:, n % 2].rearrange("p k q -> p (k q)"), src[:], ACT.Copy)\
                        .then_inc(t_free[slot], 1)
                if kind == "Z":
                    act.wait_ge(t_ready, count + 1)
                    act.activation(nullT[:], src[0:H, 0:P], ACT.Copy).then_inc(t_free[slot], 1)
                if kind == "X":
                    act.wait_ge(t_ready, count + 1)
                    act.activation(oT[:, 4 * (n % 2):4 * (n % 2) + 4].rearrange("p h q -> p (h q)"), src[:],
                                   ACT.Copy).then_inc(t_free[slot], 1)

        def place_null(layer):
            if layer == 1:
                act.wait_ge(s_ready, B * HEADS)
            for tile, part in ((k0_hi, 0), (k0_lo, 1), (k_hi, 0), (k_lo, 1)):
                act.activation(tile[:, 0:2], null_cols[:, layer, part], ACT.Copy).then_inc(null_placed, 1)

        answer(-1, None, None, 0)
        act.wait_ge(null_T, 1)
        act.activation(null_cols[:].rearrange("p l c k -> p (l c k)"), o_bank[0][:, 0:8], ACT.Copy)\
            .then_inc(act_step, 1)
        act.wait_ge(act_step, 1)
        place_null(0)
        answer(0, 0, None, 0)
        with act.Fori(1, B - 1) as s:
            answer(s, 0, 0, 0)
        answer(B - 1, 0, 0, 1)
        place_null(1)
        answer(B, 1, 0, 1)
        with act.Fori(B + 1, 2 * B - 1) as s:
            answer(s, 1, 1, 1)
        answer(2 * B - 1, 1, 1, None)
        answer(2 * B, None, 1, None)
        moe.scalar(act)

    @block.gpsimd
    def _(pool):
        pool.wait_ge(consts_ready, 1)
        sources = (((bias0, slice(0, P)), (bias1, slice(0, N))), ((toep, slice(P, N)), (toep, slice(0, N))))

        def cut(s, layer, half, g):
            wait_apart(pool, [(masked, s * HEADS + half * H + CUT * g + CUT)])
            tile, cols = sources[layer][half]
            hs = slice(CUT * g, CUT * g + CUT)
            keys = COLS[half] - 2
            pool.tensor_tensor(
                nb[half][:, hs, 2:],
                mask[:, layer, bass.ds(s - layer * B, 1), 0:keys].to_broadcast([P, CUT, keys]),
                tile[:, hs, cols], ALU.subtract).then_inc(nb_ready, 1)

        def answer(s, layer, tail_layer, next_layer):
            for kind, n, is_late in turn(s):
                b = s - 1 if is_late else s
                tile = 2 * s + 2 - n
                if kind == "stats":
                    pool.wait_ge(stats_ready, tile + 1)
                    pool.tensor_tensor(rstd[:, n:n + 1], var_e[:, n:n + 1], minus_half[:, 0:1], ALU.pow)\
                        .then_inc(rstd_ready, 1)
                if kind == "sums" and (layer if n == 1 else next_layer) == 1:
                    pool.wait_ge(norms_ready, tile - 2 * B + 1)
                    for columns in (slice(0, 8), slice(8, H + 1)):
                        pool.tensor_tensor(rq[:, n, columns], ss[:, n, columns], minus_half[:, columns], ALU.pow)\
                            .then_inc(rq_ready, 1)
                if kind == "h":
                    pool.wait_ge(mlp_dve, MLP_DVE_VAR[n])
                    pool.tensor_tensor(mlp_r[:], mlp_var[:], minus_half[:, 0:2], ALU.pow).then_inc(mlp_pool, 1)
                if kind == "W":
                    pool.wait_ge(out_stats, b * 2 + n + 1)
                    pool.tensor_tensor(out_r[:, n:n + 1], out_var[:, n:n + 1], minus_half[:, 0:1], ALU.pow)\
                        .then_inc(out_rstd, 1)
                if kind == "S" and isinstance(s, int) and s == 0 and n < H // CUT:
                    pool.wait_ge(bias_cut, 2)
                    cut(0, 0, 1, n)
                if kind == "S" and n % CUT == CUT - 1 and next_layer is not None and not (isinstance(s, int) and s < 0):
                    half, g = divmod(n // CUT, H // CUT)
                    if isinstance(s, int) and s == B - 1 and n == CUT - 1:
                        pool.wait_ge(toep_loaded, 16)
                    cut(s + 1, next_layer, half, g)

        answer(-1, None, None, 0)
        pool.wait_ge(null_ready, 1)
        pool.tensor_tensor(null_s[:, 1:2], null_s[:, 0:1], minus_half[0:2, 0:1], ALU.pow).then_inc(null_scaled, 1)
        pool.wait_ge(consts_ready, CONSTS)
        for half, tile in enumerate((bias0, bias1)):
            pool.wait_ge(loaded[f"bias{half}"], 16)
            pool.affine_select(out=tile[:, :, half * P:half * P + P], in_=tile[:, :, half * P:half * P + P],
                               compare_op=ALU.is_ge, fill=-FAR, base=0, pattern=[[0, H], [-1, P]],
                               channel_multiplier=1).then_inc(bias_cut, 1)
        pool.wait_ge(bias_cut, 1)
        for g in range(H // CUT):
            cut(0, 0, 0, g)
        answer(0, 0, None, 0)
        with pool.Fori(1, B - 1) as s:
            answer(s, 0, 0, 0)
        answer(B - 1, 0, 0, 1)
        answer(B, 1, 0, 1)
        with pool.Fori(B + 1, 2 * B - 1) as s:
            answer(s, 1, 1, 1)
        answer(2 * B - 1, 1, 1, None)
        answer(2 * B, None, 1, None)
        moe.gpsimd(pool)

    @block.vector
    def _(dve):
        chain = Chain(dve, dve_step)
        dve.memset(minus_half[:], -0.5).then_inc(consts_ready, 1)
        dve.memset(table[:], -FAR).then_inc(masked, HEADS)
        dve.memset(nb[0][:, :, 0:2], FAR).then_inc(consts_ready, 1)
        dve.memset(nb[1][:, :, 0:2], FAR).then_inc(consts_ready, 1)

        def null_norm():
            dve.wait_ge(loaded["attn"], 16 * ATTN_LOADS)
            chain(dve.tensor_tensor(k_gain[:], qk_scale[:, 0], qk_scale[:, 1], ALU.mult))
            chain.settle()
            chain(dve.tensor_scalar(k_gain[:], k_gain[:], -8.0, None, ALU.mult))
            chain(dve.tensor_tensor(null_k[:, 0], null_kv[:], null_kv[:], ALU.mult))
            chain.settle()
            chain(dve.tensor_reduce(null_s[:, 0:1], null_k[:, 0], AX.X, ALU.add))
            chain.settle()
            dve.tensor_scalar(null_s[:, 0:1], null_s[:, 0:1], 1e-24, None, ALU.max).then_inc(null_ready, 1)

        def split_weights(layer):
            if layer == 0:
                dve.wait_ge(loaded["start"], 64)
            else:
                dve.wait_ge(loaded["attn"], 16 * ATTN_LOADS)
            dve.wait_ge(loaded[f"wqkv{layer}"], 32)
            chain(dve.tensor_scalar(wqkv[:], wqkv[:], gain_in[:, layer:layer + 1], None, ALU.mult))
            chain.settle()
            chain(dve.tensor_copy(w_hi[layer][:], wqkv[:]))
            chain.settle()
            dve.tensor_tensor(w_lo[layer][:], wqkv[:], w_hi[layer][:].bitcast(F32), ALU.subtract)\
                .then_inc(w_staged, 1)

        def null_rows():
            chain(dve.tensor_scalar(null_k[:, 0], null_kv[:], -0.125, None, ALU.mult))
            dve.wait_ge(null_scaled, 1)
            chain(dve.scalar_tensor_tensor(null_k[:, 1], null_kv[:], null_s[:, 1:2], k_gain[0:2], ALU.mult,
                                           ALU.mult))
            chain.settle()
            twice = null_k[:].unsqueeze(2).to_broadcast([2, 2, 2, DH])
            chain(dve.tensor_copy(null_split[:, :, 0:2], twice))
            chain.settle()
            dve.tensor_tensor(null_split[:, :, 2:4], twice, null_split[:, :, 0:2].bitcast(F32), ALU.subtract)\
                .then_inc(null_ready, 1)

        def masks():
            dve.wait_ge(loaded["start"], 64)
            for layer in range(2):
                dve.tensor_scalar(mask[:, layer], mask_u8[:, layer], -FAR, FAR, ALU.mult, ALU.add)\
                    .then_inc(consts_ready, 1)

        def x_tile(index):
            return x_sb[:, bass.ds(index, 1), :].rearrange("p a d -> p (a d)")

        def null_column(layer):
            dve.wait_ge(masked, (layer * B + 1) * HEADS)
            for half in range(2):
                chain(dve.tensor_scalar(nb[half][:, :, 0], null_bias[:, layer], -1.0, None, ALU.mult))
            chain.settle()

        def q_low(tile, c):
            hs = slice(c * 8, c * 8 + 8)
            dve.wait_ge(q_hi, 2 * tile + c + 1)
            dve.tensor_tensor(q_split[:, hs, 1], qn[:, hs], q_split[:, hs, 0].bitcast(F32), ALU.subtract)\
                .then_inc(q_split_ready, 1)

        def answer(s, layer, tail_layer, next_layer):
            for kind, n, is_late in turn(s):
                b = s - 1 if is_late else s
                tile = 2 * s + 2 - n
                lay = layer if n == 1 else next_layer
                if kind in ("xn", "q", "T"):
                    count, pairs, slot = T_RING.use(s, kind, n, is_late)
                    src = t_bank[slot]
                if kind in ("q0", "q1", "W"):
                    count, pairs, slot = P_RING.use(s, kind, n, is_late)
                    src = p_bank[slot]
                before = (s - 1, 0) if n == 1 else (s, 1)
                first = isinstance(s, int) and s < 0
                if kind == "stats":
                    dve.wait_ge(loaded["x"], 16)
                    x_t = x_tile(tile - lay * 2 * B)
                    chain(dve.bn_stats(stats[:], x_t))
                    wait_apart(dve, [(dve_step, chain.base + chain.n)])
                    chain(dve.bn_aggr(mv[:, n], stats[:]))
                    chain.settle()
                    dve.tensor_scalar(var_e[:, n:n + 1], mv[:, n, 1:2], EPS, None, ALU.add)\
                        .then_inc(stats_ready, 1)
                if kind == "norm":
                    dve.wait_ge(rstd_ready, tile + 1)
                    dve.tensor_scalar(xn[:, n], x_tile(tile - lay * 2 * B), mv[:, n, 0:1], rstd[:, n:n + 1],
                                      ALU.subtract, ALU.mult).then_inc(xn_ready, 1)
                if kind == "xn":
                    dve.wait_ge(xn_hi, tile + 1)
                    dve.tensor_tensor(xnT_lo[:, n], src[:, 0:P], xnT_hi[:, n].bitcast(F32), ALU.subtract)\
                        .then_inc(t_free[slot], 1)
                if kind in ("q0", "q1") and lay == 0:
                    c = int(kind[1])
                    hs = slice(c * 8, c * 8 + 8)
                    dve.wait_ge(q_hi, tile * 2 + c + 1)
                    dve.tensor_tensor(q_split[:, hs, 1], src[:].rearrange("p (h d) -> p h d", d=DH),
                                      q_split[:, hs, 0].bitcast(F32), ALU.subtract).then_inc(p_free[slot], 1)
                if kind == "sums" and lay == 1:
                    dve.wait_ge(sq_done, (tile - 2 * B) * 3 + 3)
                    chain(dve.tensor_reduce(ss[:, n], sq[:].rearrange("p (h d) -> p h d", d=DH), AX.X, ALU.add))
                    chain.settle()
                    dve.tensor_scalar(ss[:, n], ss[:, n], 1e-24, None, ALU.max).then_inc(norms_ready, 1)
                if kind == "h":
                    dve.wait_ge(loaded["mlp"], 16 * 9)
                    dve.wait_ge(t_ready, T_RING.use(s, kind, n)[0] + 1)
                    pairs, slot = T_RING.use(s, kind, n)[1:]
                    flat_h = mh.rearrange("p n d -> p (n d)")
                    if n == 0:
                        dve.tensor_copy(flat_h, t_bank[slot][:, 0:2 * D]).then_inc(t_free[slot], 1)
                    else:
                        dve.tensor_tensor(mh, t_bank[slot][:, 0:2 * D].rearrange("p (n d) -> p n d", d=D),
                                          mlp_rows[:, 2].unsqueeze(1).to_broadcast([P, 2, D]), ALU.add)\
                            .then_inc(t_free[slot], 1)
                    dve.wait_ge(t_free[slot], pairs + 1 + CREDIT)
                    for c in range(2):
                        chain(dve.bn_stats(out_st[:], mh[:, c]))
                        chain.settle()
                        chain(dve.bn_aggr(mlp_mv[:, c], out_st[:]))
                        chain.settle()
                    dve.tensor_scalar(mlp_var[:], mlp_mv[:, :, 1], EPS, None, ALU.add).then_inc(mlp_dve, 1)
                if kind == "hn":
                    dve.wait_ge(mlp_pool, n + 1)
                    for c in range(2):
                        chain(dve.tensor_scalar(mh[:, c], mh[:, c], mlp_mv[:, c, 0:1], mlp_r[:, c:c + 1],
                                                ALU.subtract, ALU.mult))
                    chain.settle()
                    dve.tensor_tensor(mh, mh, mlp_rows[:, n].unsqueeze(1).to_broadcast([P, 2, D]), ALU.mult)\
                        .then_inc(mlp_dve, 1)
                if kind == "hs":
                    dve.wait_ge(mlp_act, n + 1)
                    chain(dve.tensor_scalar(me, me, 1.0, None, ALU.add))
                    chain.settle()
                    chain(dve.reciprocal(me, me))
                    chain.settle()
                    dve.tensor_tensor(mh, mh, me, ALU.mult).then_inc(mlp_dve, 1)
                if kind == "ht":
                    count, _, slot = T_RING.use(s, kind, n)
                    dve.wait_ge(t_ready, count + 1)
                    dve.tensor_copy(mhT, t_bank[slot][:, 0:N]).then_inc(t_free[slot], 1)
                if kind == "table":
                    count, _, slot = T_RING.use(s, kind, n)
                    dve.wait_ge(t_ready, count + 1)
                    dve.wait_ge(masked, HEADS)
                    dve.tensor_scalar(table[:, 0:N], t_bank[slot][0:H, 0:N], b2[:], None, ALU.add)\
                        .then_inc(t_free[slot], 1)
                if kind == "w1":
                    split_weights(1)
                if kind == "apply":
                    if lay == 0:
                        dve.wait_ge(kv_copied, tile + 1)
                        if not first:
                            dve.wait_ge(k_hi_done, tile)
                        dve.tensor_scalar(kn[:], kv[:, n, 0:DH], -0.125, None, ALU.mult).then_inc(qn_ready, 1)
                    else:
                        if not (isinstance(s, int) and s == B - 1):
                            dve.wait_ge(q_hi, 2 * tile)
                            dve.wait_ge(q_split_ready, 2 * (tile - 2 * B))
                        for c in range(2):
                            dve.wait_ge(rq_ready, 2 * (tile - 2 * B) + c + 1)
                            if c == 1:
                                dve.wait_ge(k_hi_done, tile)
                                dve.scalar_tensor_tensor(kn[:], kv[:, n, 0:DH], rq[:, n, H:H + 1],
                                                         k_gain[:], ALU.mult, ALU.mult).then_inc(qn_ready, 1)
                            _, _, slot = P_RING.use(s, f"q{c}", n)
                            hs = slice(c * 8, c * 8 + 8)
                            dve.tensor_tensor(qn[:, hs], p_bank[slot][:].rearrange("p (h d) -> p h d", d=DH),
                                              rq[:, n, hs].unsqueeze(2).to_broadcast([P, 8, DH]), ALU.mult)\
                                .then_inc(p_free[slot], 1)
                if kind == "split":
                    if lay == 1:
                        q_low(tile, 0)
                    dve.wait_ge(k_hi_done, tile + 1)
                    dve.tensor_tensor(k_split[:, 2:4], kn[:].unsqueeze(1).to_broadcast([P, 2, DH]),
                                      k_split[:, 0:2].bitcast(F32), ALU.subtract).then_inc(k_split_ready, 1)
                    if lay == 1:
                        q_low(tile, 1)
                if kind == "q" and n % 2 == 1:
                    dve.wait_ge(t_ready, count + 1)
                    dve.tensor_copy(qT[:, n // 4, 4 * (n % 4):4 * (n % 4) + 4].rearrange("p h q -> p (h q)"), src[:])\
                        .then_inc(t_free[slot], 1)
                if kind == "S":
                    half, h = divmod(n, H)
                    waits = [(s_ready, s * HEADS + n + 1), (probs, s * HEADS + n - 3 + CREDIT)]
                    if first_turn(s) and n < 4:
                        waits.pop()
                    if h % CUT == 0:
                        waits.append((nb_ready, (s * HEADS + n) // CUT + 1 if isinstance(s, int) else
                                      s * (HEADS // CUT) + n // CUT + 1))
                    wait_apart(dve, waits)
                    dve.tensor_tensor_reduce(t_sb[:, n % 4, 0:COLS[half]], s_bank[n % 2][:, 0:COLS[half]],
                                             nb[half][:, h], 1.0, 3e38, ALU.add, ALU.min,
                                             low[:, n:n + 1]).then_inc(masked, 1)
                if kind == "T" and n not in TURNED_BY_ACT:
                    dve.wait_ge(t_ready, count + 1)
                    if not (first_turn(s) and n < 2):
                        dve.wait_ge(v_done, b * len(QUADS) + n - 1 + CREDIT)
                    dve.tensor_copy(pT[:, n % 2].rearrange("p k q -> p (k q)"), src[:]).then_inc(t_free[slot], 1)
                if kind == "Y":
                    half = n
                    dve.wait_ge(probs, b * HEADS + half * H + H + CREDIT)
                    hs = slice(half * H, half * H + H)
                    chain(dve.reciprocal(recip[:, hs], total[:, hs]))
                    chain.settle()
                    for c in range(2):
                        dve.wait_ge(o_done, b * 4 + half * 2 + c + 1)
                        r = recip[:, half * H + c * 8:half * H + c * 8 + 8].unsqueeze(2).to_broadcast([P, 8, DH])
                        dve.tensor_tensor(o_sb[:, c * 512:c * 512 + 512].rearrange("p (h d) -> p h d", d=DH),
                                          o_bank[c][:].rearrange("p (h d) -> p h d", d=DH), r, ALU.mult)\
                            .then_inc(o_ready, 1)
                if kind == "W":
                    half = n
                    dve.wait_ge(p_ready, count + 1)
                    chain(dve.bn_stats(out_st[:], src[:, 0:D]))
                    wait_apart(dve, [(dve_step, chain.base + chain.n)])
                    chain(dve.bn_aggr(out_mv[:, half], out_st[:]))
                    chain.settle()
                    dve.tensor_scalar(out_var[:, half:half + 1], out_mv[:, half, 1:2], EPS, None, ALU.add)\
                        .then_inc(out_stats, 1)
                if kind == "out":
                    half = n
                    _, pairs, slot = P_RING.use(s, "W", half, is_late)
                    src = p_bank[slot]
                    dve.wait_ge(out_rstd, b * 2 + half + 1)
                    dve.tensor_scalar(ln_sb[:, half], src[:, 0:D], out_mv[:, half, 0:1], out_r[:, half:half + 1],
                                      ALU.subtract, ALU.mult).then_inc(p_free[slot], 1)
                    dve.wait_ge(p_free[slot], pairs + 1 + CREDIT)
                    lay = tail_layer if is_late else layer
                    chain(dve.tensor_tensor(ln_sb[:, half], ln_sb[:, half], gain_out[:, lay], ALU.mult))
                    chain.settle()
                    x_t = x_tile(2 * b + half - lay * 2 * B)
                    chain(dve.tensor_tensor(x_t, x_t, ln_sb[:, half], ALU.add))
                    chain.settle()

        split_weights(0)
        answer(-1, None, None, 0)
        masks()
        null_norm()
        null_rows()
        null_column(0)
        answer(0, 0, None, 0)
        with dve.Fori(1, B - 1) as s:
            chain.enter(s - 1, DVE_CHAIN[0])
            answer(s, 0, 0, 0)
        chain.leave(B - 2)
        answer(B - 1, 0, 0, 1)
        null_column(1)
        answer(B, 1, 0, 1)
        with dve.Fori(B + 1, 2 * B - 1) as s:
            chain.enter(s - B - 1, DVE_CHAIN[1])
            answer(s, 1, 1, 1)
        chain.leave(B - 2)
        answer(2 * B - 1, 1, 1, None)
        answer(2 * B, None, 1, None)
        moe.vector(dve, chain)

    @block.tensor
    def _(pe):
        pe.wait_ge(loaded["start"], 64)

        def work(s, layer, tail_layer, next_layer):
            for kind, n, is_late in turn(s):
                b = s - 1 if is_late else s
                tile = 2 * s + 2 - n
                lay = layer if n == 1 else next_layer
                if kind in T_RING.kinds:
                    count, pairs, slot = T_RING.use(s, kind, n, is_late)
                    dst = t_bank[slot]
                    if kind == "q":
                        tile, lay = 2 * s + 2 - n // 4, layer if n // 4 == 1 else next_layer
                    pe.wait_ge(t_free[slot], pairs + CREDIT)
                if kind in P_RING.kinds:
                    count, pairs, slot = P_RING.use(s, kind, n, is_late)
                    dst = p_bank[slot]
                    pe.wait_ge(p_free[slot], pairs + CREDIT)
                if kind == "h":
                    pe.wait_ge(loaded["mlp"], 16 * 9)
                    for c in range(2):
                        lhs, rhs = (pos_rows[:, c * P:c * P + P], w0b0[:]) if n == 0 else \
                            (mhT[:, c * P:c * P + P], w1[:])
                        if n == 1:
                            _, pairs, copied = T_RING.use(s, "ht", 0)
                            pe.wait_ge(t_free[copied], pairs + 1 + CREDIT)
                        ins = pe.matmul(dst[:, c * D:c * D + D], lhs, rhs, start=True, stop=True)
                    ins.then_inc(t_ready, 1)
                if kind == "ht":
                    pe.wait_ge(mlp_dve, MLP_DVE_SILU[n])
                    for c in range(2):
                        ins = pe.transpose(dst[:, c * P:c * P + P], mh[:, c], ident[:])
                    ins.then_inc(t_ready, 1)
                if kind == "table":
                    _, pairs, copied = T_RING.use(s, "ht", 1)
                    pe.wait_ge(t_free[copied], pairs + 1 + CREDIT)
                    pe.matmul(dst[0:H, 0:N], w2[:], mhT, start=True, stop=True).then_inc(t_ready, 1)
                if kind == "xn":
                    pe.wait_ge(xn_ready, tile + 1)
                    pe.transpose(dst[:, 0:P], xn[:, n], ident[:]).then_inc(t_ready, 1)
                if kind in ("kv", "q0", "q1"):
                    if kind == "kv":
                        _, pairs, slot = T_RING.use(s, "xn", n)
                        pe.wait_ge(t_free[slot], pairs + 1 + CREDIT)
                        pe.wait_ge(w_staged, lay + 1)
                    start, width = {"q0": (0, 512), "q1": (512, 512), "kv": (INNER, P)}[kind]
                    for i, (lhs, rhs) in enumerate(((xnT_hi, w_hi), (xnT_hi, w_lo), (xnT_lo, w_hi))):
                        ins = pe.matmul(dst[:, 0:width], lhs[:, n], rhs[lay][:, start:start + width],
                                        start=(i == 0), stop=(i == 2))
                    ins.then_inc(p_ready, 1)
                if kind == "q":
                    g = n % 4
                    if lay == 0:
                        _, pairs, slot = P_RING.use(s, f"q{g // 2}", n // 4)
                        pe.wait_ge(p_free[slot], pairs + 1 + CREDIT)
                    else:
                        pe.wait_ge(q_split_ready, 2 * (tile - 2 * B) + g // 2 + 1)
                    for j in range(4):
                        ins = pe.transpose(dst[:, j * P:j * P + P],
                                           q_split[:, 4 * g + j].rearrange("p a d -> p (a d)").bitcast(F32), ident[:])
                    ins.then_inc(t_ready, 1)
                if kind == "K":
                    pe.wait_ge(k_split_ready, tile + 1)
                    for c in range(2):
                        ins = pe.transpose(dst[:, c * P:c * P + P],
                                           k_split[:, 2 * c:2 * c + 2].rearrange("p a d -> p (a d)").bitcast(F32),
                                           ident[:])
                    ins.then_inc(t_ready, 1)
                if kind == "S":
                    half, h = divmod(n, H)
                    if h == 0:
                        where, m = (s - 1, 0) if half == 0 else (s, 1)
                        for wanted in (("q", 4 * m + 2), ("q", 4 * m + 3), ("K", m)):
                            _, pairs, slot = T_RING.use(where, *wanted)
                            pe.wait_ge(t_free[slot], pairs + 1 + CREDIT)
                        pe.wait_ge(k_placed, 2 * s + half + 1)
                        if half == 1:
                            pe.wait_ge(k0_copied, 2 * s + 2)
                    keys_hi, keys_lo = ((k0_hi, k0_lo), (k_hi, k_lo))[half]
                    pe.wait_ge(masked, s * HEADS + HEADS + max(n - 1, 0))
                    dst = s_bank[n % 2][:, 0:COLS[half]]
                    pe.matmul(dst, qT[:, half, h], keys_hi[:], start=True, stop=False)
                    pe.matmul(dst, qT[:, half, h], keys_lo[:], start=False, stop=True)\
                        .then_inc(s_ready, 1)
                if kind == "T":
                    half, first, k = QUADS[n]
                    pe.wait_ge(probs, b * HEADS + first + k + CREDIT)
                    for j in range(4):
                        h, kb = (first + j, 0) if half == 0 else (first - H + j // 2, j % 2)
                        ins = pe.transpose(dst[:, j * P:j * P + P], prob[half][:, h, 2 + kb * P:2 + kb * P + P],
                                           ident[:])
                    ins.then_inc(t_ready, 1)
                if kind == "V":
                    half, first, k = QUADS[n]
                    where = s - 1 if is_late and not late("T", n) else s
                    _, pairs, slot = T_RING.use(where, "T", n, late("T", n))
                    pe.wait_ge(t_free[slot], pairs + 1 + CREDIT)
                    if first % H == 0:
                        pe.wait_ge(v_placed, 2 * b + half + 1)
                    for j in range(4):
                        h, kb = (first + j, 0) if half == 0 else (first - H + j // 2, j % 2)
                        bk = o_bank[h // 8]
                        if h % 8 == 0 and kb == 0:
                            pe.wait_ge(o_ready, b * 4 + half * 2 + CREDIT)
                        ins = pe.matmul(bk[:, (h % 8) * DH:(h % 8) * DH + DH], pT[:, n % 2, j], v_sb[:, kb],
                                        start=(h % 8 == 0 and kb == 0), stop=False, skip_group_check=True)
                    ins.then_inc(v_done, 1)
                if kind == "Z":
                    pe.wait_ge(probs, b * HEADS + n * H + H + CREDIT)
                    pe.transpose(dst[0:H, 0:P], prob[n][:, :, 0], ident[:]).then_inc(t_ready, 1)
                if kind == "Y":
                    where = s - 1 if is_late and not late("Z", n) else s
                    _, pairs, slot = T_RING.use(where, "Z", n, late("Z", n))
                    pe.wait_ge(t_free[slot], pairs + 1 + CREDIT)
                    for c in range(2):
                        pe.matmul(o_bank[c][:], nullT[:], null_v[:, c * 8:c * 8 + 8].rearrange("h a d -> h (a d)"),
                                  start=False, stop=True, skip_group_check=True).then_inc(o_done, 1)
                if kind == "X":
                    half, c = divmod(n, 2)
                    pe.wait_ge(o_ready, b * 4 + half * 2 + c + 1 + CREDIT)
                    for j in range(4):
                        ins = pe.transpose(dst[:, j * P:j * P + P], o_sb[:, (4 * c + j) * P:(4 * c + j) * P + P],
                                           ident[:])
                    ins.then_inc(t_ready, 1)
                if kind == "W":
                    lay = tail_layer if is_late else layer
                    pe.wait_ge(loaded["wo"], 32)
                    for c in range(2):
                        _, pairs, slot = T_RING.use(s, "X", 2 * n + c, is_late)
                        pe.wait_ge(t_free[slot], pairs + 1 + CREDIT)
                    for j in range(H // 2):
                        ins = pe.matmul(dst[:, 0:D], oT[:, j], wo[lay][:, j], start=(j == 0),
                                        stop=(j == H // 2 - 1))
                    ins.then_inc(p_ready, 1)

        work(-1, None, None, 0)
        pe.wait_ge(null_ready, 2)
        for layer in range(2):
            for c in range(2):
                ins = pe.transpose(o_bank[0][:, 4 * layer + 2 * c:4 * layer + 2 * c + 2],
                                   null_split[:, layer, 2 * c:2 * c + 2].rearrange("p a d -> p (a d)").bitcast(F32),
                                   ident[0:2, 0:2])
        ins.then_inc(null_T, 1)
        pe.wait_ge(null_placed, 4)
        work(0, 0, None, 0)
        with pe.Fori(1, B - 1) as s:
            work(s, 0, 0, 0)
        work(B - 1, 0, 0, 1)
        pe.wait_ge(null_placed, 8)
        work(B, 1, 0, 1)
        with pe.Fori(B + 1, 2 * B - 1) as s:
            work(s, 1, 1, 1)
        work(2 * B - 1, 1, 1, None)
        work(2 * B, None, 1, None)
        moe.tensor(pe)


CREDIT = 1
ATTN_LOADS = 9
MLP_DVE_VAR, MLP_DVE_H, MLP_DVE_SILU = (1, 4), (2, 5), (3, 6)
DVE_CHAIN = (14, 16)


def first_turn(s):
    return isinstance(s, int) and s == 0


class Moe:

    WEIGHT_WORDS = 2 * (2 * DOWN_TILES * P + DOWN_TILES * D + 2 * E) + B + B * P + EXPERT_TILES * P + E * E

    def __init__(self, sb, sem, bank, ident, x_sb):
        self.bank, self.ident, self.x_sb = bank, ident, x_sb
        self.w_raw = [sb(f"moe_w{i}", [P, 2, DOWN_TILES, P]) for i in range(2)]
        self.w_down = [sb(f"moe_down{i}", [P, DOWN_TILES, D]) for i in range(2)]
        self.w_token = [sb(f"moe_wt{i}", [D, E]) for i in range(2)]
        self.w_g = [sb(f"moe_wg{i}", [G, E]) for i in range(2)]
        self.gT = sb("moe_gT", [G, B])
        self.g_rep = sb("moe_g_rep", [G, B, P])
        self.sel_raw = sb("moe_sel_raw", [2 * E, EXPERT_TILES, P])
        self.tri = sb("moe_tri", [P, E, E])
        self.loaded = sem("moe_loaded")
        self.attended = sem("attended")
        self.w_hi_done, self.w_ready = sem("moe_w_hi_done"), sem("moe_w_ready")
        self.consts = sem("moe_consts")
        self.x_turned, self.x_copied, self.x_hi, self.x_lo = (sem("moe_" + n) for n in
                                                              ("x_turned", "x_copied", "x_hi", "x_lo"))
        self.logits, self.shifted, self.exps = sem("moe_logits"), sem("moe_shifted"), sem("moe_exps")
        self.routed, self.w_turned, self.w_copied = sem("moe_routed"), sem("moe_w_turned"), sem("moe_w_copied")
        self.gate, self.up, self.weight = sem("moe_gate"), sem("moe_up"), sem("moe_weight")
        self.leaked, self.hidden = sem("moe_leaked"), sem("moe_hidden")
        self.y, self.added = sem("moe_y"), sem("moe_added")
        self.out_turned, self.out_ready = sem("moe_out_turned"), sem("moe_out_ready")

    def allocate(self, sb):
        self.w_hi = [sb(f"moe_w_hi{i}", [P, 2, DOWN_TILES, P], F32R) for i in range(2)]
        self.w_lo = [sb(f"moe_w_lo{i}", [P, 2, DOWN_TILES, P], F32R) for i in range(2)]
        self.sel = sb("moe_sel", [2 * E, EXPERT_TILES, P], F32R)
        self.xT = sb("moe_xT", [P, B * N])
        self.xT_hi = sb("moe_xT_hi", [P, B * N], F32R)
        self.xT_lo = sb("moe_xT_lo", [P, B * N], F32R)
        self.score = sb("moe_score", [P, TILES, E])
        self.red = sb("moe_red", [P, TILES])
        self.beats = sb("moe_beats", [P, TILES, E, E])
        self.ties = sb("moe_ties", [P, TILES, E, E])
        self.rank = sb("moe_rank", [P, TILES, E])
        self.w_split = sb("moe_w_split", [P, TILES, 2 * E], F32R)
        self.wT = sb("moe_wT", [2 * E, B * N], F32R)
        self.leak = sb("moe_leak", [P, 2, HALF_T])
        self.hid = sb("moe_hid", [P, DOWN_TILES, HALF_T])

    def load(self, sp, a):
        def dma(dst, src):
            sp.dma_start(dst, src).then_inc(self.loaded, 16)

        for i, name in ((0, "L2_cond_"), (1, "L3_cond_")):
            for n, which in enumerate(("gate", "up")):
                dst = self.w_raw[i][:, n].rearrange("p t m -> p (t m)")
                dma(dst[:, 0:E * M].rearrange("p (e m) -> p e m", e=E),
                    a[name + "w_" + which].rearrange("e h m -> h e m"))
                dma(dst[:, E * M:], a[name + "sw_" + which])
            dma(self.w_down[i][:, 0:EXPERT_TILES],
                a[name + "w_down"].rearrange("e m d -> (e m) d").rearrange("(j p) d -> p j d", p=P))
            dma(self.w_down[i][:, EXPERT_TILES], a[name + "sw_down"])
        for i, name in ((0, "L2_cond_"), (1, "L3_cond_")):
            dma(self.w_token[i][:], a[name + "wtT"])
            dma(self.w_g[i][:], a[name + "wgT"])
        dma(self.gT[:], a["gT"])
        dma(self.sel_raw[:], a["sel"])
        dma(self.tri[:], a["tri"].partition_broadcast(P))

    N_LOADS = 12 + 4 + 3

    def scalar(self, act):
        bank = self.bank
        for layer in range(2):
            if layer == 0:
                for c in range(2):
                    act.wait_ge(self.x_turned, c + 1)
                    act.activation(self.xT_hi[:, c * 512:c * 512 + 512], bank[c][:], ACT.Copy).then_inc(self.x_hi, 1)
            else:
                act.wait_ge(self.added, 2 + CREDIT)
                act.activation(self.xT_hi[:], self.xT[:], ACT.Copy).then_inc(self.x_hi, 2)
            if layer == 0:
                act.wait_ge(self.loaded, 16 * self.N_LOADS)
                act.activation(self.w_hi[0][:], self.w_raw[0][:], ACT.Copy).then_inc(self.w_hi_done, 1)
            act.wait_ge(self.shifted, layer + 1)
            act.activation(self.score[:], self.score[:], ACT.Exp, scale=0.5).then_inc(self.exps, 1)
            if layer == 0:
                act.activation(self.w_hi[1][:], self.w_raw[1][:], ACT.Copy).then_inc(self.w_hi_done, 1)
            with act.Fori(2 * layer, 2 * layer + 2) as v:
                for m in range(DOWN_TILES):
                    act.wait_ge(self.gate, v * DOWN_TILES + m + 1)
                    act.activation(self.leak[:, m % 2], bank[4 + m % 2][:], ACT.Copy, scale=0.01)\
                        .then_inc(self.leaked, 1)
        for c in range(2):
            act.wait_ge(self.out_turned, c + 1)
            act.activation(self.leak[:, c], bank[c][:], ACT.Copy).then_inc(self.out_ready, 1)

    def prepare(self, dve, chain):
        dve.wait_ge(self.loaded, 16 * self.N_LOADS)
        dve.tensor_copy(self.g_rep[:], self.gT[:].unsqueeze(2).to_broadcast([G, B, P])).then_inc(self.consts, 1)
        dve.tensor_copy(self.sel[:], self.sel_raw[:]).then_inc(self.consts, 1)

    def vector(self, dve, chain):
        bank, score, red = self.bank, self.score, self.red

        def over(x):
            return x.unsqueeze(2).to_broadcast([P, TILES, E])

        def weights_low(layer):
            dve.wait_ge(self.w_hi_done, layer + 1)
            dve.tensor_tensor(self.w_lo[layer][:], self.w_raw[layer][:], self.w_hi[layer][:].bitcast(F32),
                              ALU.subtract).then_inc(self.w_ready, 1)

        chain.settle()
        dve.sem_inc(self.attended, 1)
        for layer in range(2):
            if layer == 0:
                for c in range(2):
                    cols = slice(c * 512, c * 512 + 512)
                    dve.wait_ge(self.x_hi, c + 1)
                    dve.tensor_copy(self.xT[:, cols], bank[c][:]).then_inc(self.x_copied, 1)
            dve.wait_ge(self.x_hi, 2 * layer + 2)
            if layer == 0:
                dve.wait_ge(self.x_copied, 2)
            dve.tensor_tensor(self.xT_lo[:], self.xT[:], self.xT_hi[:].bitcast(F32), ALU.subtract)\
                .then_inc(self.x_lo, 1)
            if layer == 0:
                self.prepare(dve, chain)
                weights_low(0)
            dve.wait_ge(self.logits, layer + 1)
            lg = bank[2][:, 0:TILES * E].rearrange("p (t e) -> p t e", e=E)
            chain(dve.tensor_reduce(red[:], lg, AX.X, ALU.max))
            chain.settle()
            dve.tensor_tensor(score[:], lg, over(red[:]), ALU.subtract).then_inc(self.shifted, 1)
            dve.wait_ge(self.exps, layer + 1)
            chain(dve.tensor_reduce(red[:], score[:], AX.X, ALU.add))
            chain.settle()
            chain(dve.reciprocal(red[:], red[:]))
            chain.settle()
            chain(dve.tensor_tensor(score[:], score[:], over(red[:]), ALU.mult))
            chain.settle()
            mine = score[:].unsqueeze(3).to_broadcast([P, TILES, E, E])
            others = score[:].unsqueeze(2).to_broadcast([P, TILES, E, E])
            chain(dve.tensor_tensor(self.beats[:], others, mine, ALU.is_gt))
            chain(dve.tensor_tensor(self.ties[:], others, mine, ALU.is_equal))
            chain.settle()
            chain(dve.tensor_tensor(self.ties[:], self.ties[:],
                                    self.tri[:].unsqueeze(1).to_broadcast([P, TILES, E, E]), ALU.mult))
            chain.settle()
            chain(dve.tensor_tensor(self.beats[:], self.beats[:], self.ties[:], ALU.add))
            chain.settle()
            chain(dve.tensor_reduce(self.rank[:], self.beats[:], AX.X, ALU.add))
            chain.settle()
            chain(dve.tensor_scalar(self.rank[:], self.rank[:], 2.0, None, ALU.is_lt))
            chain.settle()
            chain(dve.tensor_tensor(score[:], score[:], self.rank[:], ALU.mult))
            chain.settle()
            chain(dve.tensor_reduce(red[:], score[:], AX.X, ALU.add))
            chain.settle()
            chain(dve.tensor_scalar(red[:], red[:], 1e-20, None, ALU.add))
            chain.settle()
            chain(dve.reciprocal(red[:], red[:]))
            chain.settle()
            chain(dve.tensor_tensor(score[:], score[:], over(red[:]), ALU.mult))
            chain.settle()
            chain(dve.tensor_copy(self.w_split[:, :, 0:E], score[:]))
            chain.settle()
            dve.tensor_tensor(self.w_split[:, :, E:], score[:], self.w_split[:, :, 0:E].bitcast(F32), ALU.subtract)\
                .then_inc(self.routed, 1)
            for c in range(2):
                dve.wait_ge(self.w_turned, 2 * layer + c + 1)
                dve.tensor_copy(self.wT[:, c * 512:c * 512 + 512], bank[2 + c][0:2 * E, :])\
                    .then_inc(self.w_copied, 1)
            if layer == 0:
                weights_low(1)
            with dve.Fori(2 * layer, 2 * layer + 2) as v:
                chain.enter(v - 2 * layer, 2 * DOWN_TILES - 1)
                for m in range(DOWN_TILES):
                    hid = self.hid[:, m]
                    dve.wait_ge(self.leaked, v * DOWN_TILES + m + 1)
                    chain(dve.tensor_tensor(hid, bank[4 + m % 2][:], self.leak[:, m % 2], ALU.max))
                    chain.settle()
                    dve.wait_ge(self.up, v * DOWN_TILES + m + 1)
                    ins = dve.tensor_tensor(hid, hid, bank[6 + m % 2][:], ALU.mult)
                    if m < EXPERT_TILES:
                        chain(ins)
                        chain.settle()
                        dve.wait_ge(self.weight, v * EXPERT_TILES + m + 1)
                        ins = dve.tensor_tensor(hid, hid, bank[2 + m % 2][:], ALU.mult)
                    ins.then_inc(self.hidden, 1)
                dve.wait_ge(self.y, v + 1)
                x = self.xT[:, bass.ds((v - 2 * layer) * HALF_T, HALF_T)]
                dve.tensor_tensor(x, x, bank[0][:], ALU.add).then_inc(self.added, 1)
            chain.leave(2)

    def gpsimd(self, pool):
        pass

    def tensor(self, pe):
        bank, ident = self.bank, self.ident
        pe.wait_ge(self.attended, 1)
        for layer in range(2):
            if layer == 0:
                for t in range(TILES):
                    ins = pe.transpose(bank[t // 4][:, (t % 4) * P:(t % 4) * P + P], self.x_sb[:, t], ident[:])
                    if t % 4 == 3:
                        ins.then_inc(self.x_turned, 1)
                pe.wait_ge(self.x_copied, 2)
                pe.wait_ge(self.consts, 2)
            else:
                pe.wait_ge(self.added, 2 + CREDIT)
            for t in range(TILES):
                dst = bank[2][:, t * E:t * E + E]
                pe.matmul(dst, self.xT[:, t * P:t * P + P], self.w_token[layer][:], start=True, stop=False)
                ins = pe.matmul(dst, self.g_rep[:, t // 2], self.w_g[layer][:], start=False, stop=True)
            ins.then_inc(self.logits, 1)
            pe.wait_ge(self.routed, layer + 1)
            for t in range(TILES):
                ins = pe.transpose(bank[2 + t // 4][0:2 * E, (t % 4) * P:(t % 4) * P + P],
                                   self.w_split[:, t].bitcast(F32), ident[:])
                if t % 4 == 3:
                    ins.then_inc(self.w_turned, 1)
            pe.wait_ge(self.w_copied, 2 * layer + 2)
            pe.wait_ge(self.x_lo, layer + 1)
            pe.wait_ge(self.w_ready, layer + 1)
            with pe.Fori(2 * layer, 2 * layer + 2) as v:
                cols = bass.ds((v - 2 * layer) * HALF_T, HALF_T)

                def down(m):
                    pe.wait_ge(self.hidden, v * DOWN_TILES + m + 1 + CREDIT)
                    if m == 0:
                        pe.wait_ge(self.added, v + CREDIT)
                    return pe.matmul(bank[0][:], self.w_down[layer][:, m], self.hid[:, m], start=(m == 0),
                                     stop=(m == DOWN_TILES - 1))

                for m in range(DOWN_TILES):
                    pe.wait_ge(self.hidden, v * DOWN_TILES + max(m - 1, 0) + CREDIT)
                    for n, (base, ready) in enumerate(((4, self.gate), (6, self.up))):
                        w_hi, w_lo = self.w_hi[layer][:, n, m], self.w_lo[layer][:, n, m]
                        dst = bank[base + m % 2][:]
                        pe.matmul(dst, w_hi, self.xT_hi[:, cols], start=True, stop=False)
                        pe.matmul(dst, w_hi, self.xT_lo[:, cols], start=False, stop=False)
                        pe.matmul(dst, w_lo, self.xT_hi[:, cols], start=False, stop=True).then_inc(ready, 1)
                    if m < EXPERT_TILES:
                        pe.matmul(bank[2 + m % 2][:], self.sel[:, m], self.wT[:, cols], start=True, stop=True)\
                            .then_inc(self.weight, 1)
                    if m >= 1:
                        down(m - 1)
                down(DOWN_TILES - 1).then_inc(self.y, 1)
        pe.wait_ge(self.added, 4 + CREDIT)
        for t in range(TILES):
            ins = pe.transpose(bank[t // 4][:, (t % 4) * P:(t % 4) * P + P], self.xT[:, t * P:t * P + P], ident[:])
            if t % 4 == 3:
                ins.then_inc(self.out_turned, 1)

    def store(self, sp, out, stored):
        for c in range(2):
            sp.wait_ge(self.out_ready, c + 1)
            sp.dma_start(out.rearrange("(c t p) d -> c p t d", p=P, t=4)[c],
                         self.leak[:, c].rearrange("p (t d) -> p t d", d=D)).then_inc(stored, 16)
        sp.wait_ge(stored, 32)


def moe_arrays(g):
    arrays = {"gT": g["cond_64"].T}
    sel = np.zeros((2, E, EXPERT_TILES, 2, M), np.float32)
    for e in range(E):
        sel[:, e, e // 2, e % 2] = 1
    arrays["sel"] = sel.reshape(2 * E, EXPERT_TILES, P)
    arrays["tri"] = np.tril(np.ones((E, E), np.float32), -1)
    for name in ("L2_cond_", "L3_cond_"):
        for w in ("w_gate", "w_up", "w_down", "sw_gate", "sw_up", "sw_down"):
            arrays[name + w] = g[name + w]
        arrays[name + "wtT"] = g[name + "wt"].T
        arrays[name + "wgT"] = g[name + "wg"].T
    return arrays


def kernel(**inputs):
    import concourse.bacc as bacc
    from concourse.bass_utils import run_bass_kernel_spmd

    g = {n: np.asarray(v) for n, v in inputs.items()}
    cond = g["cond_64"]
    null_key_rows = np.zeros((2, DH), np.float32)
    null_key_rows[0] = cond[0]
    null_v_blocks = np.zeros((H, H, DH), np.float32)
    for h in range(H):
        null_v_blocks[h, h] = cond[1]
    pos_rows = np.ones((2, N), np.float32)
    pos_rows[0] = np.arange(N - 1, -1, -1)
    arrays = {
        "x": g["x"].reshape(B * N, D),
        "bias": g["fside_16xSxS_0"],
        "mask0": g["mask_BxS_bk0"],
        "mask1": g["mask_BxS_bf1"],
        "ident": np.eye(P, dtype=np.float32),
        "null_key_rows": null_key_rows,
        "null_v_blocks": null_v_blocks.reshape(H, INNER),
        "pos_rows": pos_rows,
    }
    for name in ("L0_cond_g_in", "L0_cond_null_attn_bias", "L0_cond_Wq", "L0_cond_Wkv", "L0_cond_Wo",
                 "L0_cond_g_out", "L1_cond_g_norm", "L1_cond_Wq", "L1_cond_Wkv", "L1_cond_q_scale",
                 "L1_cond_k_scale", "L1_cond_null_attn_bias", "L1_cond_w0", "L1_cond_b0", "L1_cond_g0",
                 "L1_cond_w1", "L1_cond_b1", "L1_cond_g1", "L1_cond_w2", "L1_cond_b2", "L1_cond_Wout",
                 "L1_cond_g_out"):
        arrays[name] = g[name]
    arrays.update(moe_arrays(g))
    arrays = {n: np.ascontiguousarray(v) for n, v in arrays.items()}

    nc = bacc.Bacc("TRN2", target_bir_lowering=False, num_devices=1)
    aps = {n: nc.dram_tensor("in_" + n, v.shape, mybir.dt.from_np(v.dtype), kind="ExternalInput").ap()
           for n, v in arrays.items()}
    out = nc.dram_tensor("out", (B * N, D), F32, kind="ExternalOutput").ap()
    build(nc, aps, out)
    r = run_bass_kernel_spmd(nc, [{"in_" + n: v for n, v in arrays.items()}], core_ids=[0])
    return r.results[0]["out"].reshape(B, N, D)
```
